# Optimizing a Trainium2 kernel written in Bass

```python
import numpy as np
import jax
import jax.numpy as jnp

def _softmax(x, axis=-1):
    return jax.nn.softmax(x, axis=axis)

def _gelu(x):
    return jax.nn.gelu(x, approximate=True)

def _silu(x):
    return jax.nn.silu(x)

def _sigmoid(x):
    return jax.nn.sigmoid(x)

def _layernorm(x, axis=-1, eps=1e-05):
    m = jnp.mean(x, axis=axis, keepdims=True)
    v = jnp.var(x, axis=axis, keepdims=True)
    return (x - m) / jnp.sqrt(v + eps)

def _scatter_add(tgt, idx, src, axis=0):
    return tgt.at[idx].add(src)

def _segment_sum(src, seg, n):
    return jax.ops.segment_sum(src, seg, n)
kernel_name = 'mk_flamingo_gated_d4_seqx_r8_02ba48'

def setup_inputs(seed: int=0):
    np.random.seed(seed)
    _w = jnp.asarray

    def _rec_inputs():
        import jax
        import jax.numpy as jnp
        _rk = jax.random.key(seed)
        x = -0.0002928 + 1 * jax.random.normal(jax.random.fold_in(_rk, 1), (16, 64, 256), jnp.float32)
        _lenS = 64 - jax.random.randint(jax.random.fold_in(_rk, 7), (16,), 0, max(1, 64 // 4) + 1, jnp.int32)
        _lenS2 = 64 - jax.random.randint(jax.random.fold_in(_rk, 8), (16,), 0, max(1, 64 // 4) + 1, jnp.int32)
        _ctx_2048P = jax.random.normal(jax.random.fold_in(_rk, 11), (16, 16, 256), jnp.float32)
        _ctx_2048c = jax.random.dirichlet(jax.random.fold_in(_rk, 511), 0.3 * jnp.ones((16,), jnp.float32), (16, 64))
        _ctx_2048t = jnp.einsum('bsk,bkd->bsd', _ctx_2048c, _ctx_2048P)
        _ctx_2048t = _ctx_2048t * jax.lax.rsqrt(jnp.mean(jnp.square(_ctx_2048t)) + 1e-12) * 0.953939
        ctx_2048 = -1.39393e-06 + 0.999914 * (_ctx_2048t + 0.3 * jax.random.normal(jax.random.fold_in(_rk, 611), (16, 64, 256), jnp.float32))
        itok_BxS_0_1023 = jax.random.randint(jax.random.fold_in(_rk, 12), (16, 64), 0, 128, jnp.int32)
        _validS = jnp.arange(64)[None, :] < _lenS[:, None]
        _validS2 = jnp.arange(64)[None, :] < _lenS2[:, None]
        _causal = jnp.tril(jnp.ones((64, 64), dtype=bool))
        mask_BxS2_bk0 = jnp.logical_not(jnp.broadcast_to(_validS2[:, :], (16, 64)))
        _g = jax.random.normal(jax.random.fold_in(_rk, 9001), (2, 4), jnp.float32)
        _g = jnp.sign(_g) * jnp.maximum(jnp.abs(_g), 1.0) + (_g == 0) * 1.0
        g_xattn = _g[0]
        g_ffn = _g[1]
        return (x, ctx_2048, itok_BxS_0_1023, mask_BxS2_bk0, g_xattn, g_ffn)
    x, ctx_2048, itok_BxS_0_1023, mask_BxS2_bk0, g_xattn, g_ffn = _rec_inputs()

    def _L0_xattn_setup():
        import jax, jax.numpy as jnp
        import numpy as np
        HEADS = 8
        DIM_HEAD = 64
        HIDDEN = HEADS * DIM_HEAD
        key = jax.random.key(seed)
        ks = jax.random.split(key, 5)
        b, dim, n = (4, 64, 256)
        ctx_dim, m = (64, 256)
        x = jax.random.normal(ks[0], (b, dim, n), dtype=jnp.float32)
        context = jax.random.normal(ks[1], (b, ctx_dim, m), dtype=jnp.float32)
        Wq = jax.random.normal(ks[2], (HIDDEN, dim), dtype=jnp.float32) / np.sqrt(dim).astype(np.float32)
        Wkv = jax.random.normal(ks[3], (2 * HIDDEN, ctx_dim), dtype=jnp.float32) / np.sqrt(ctx_dim).astype(np.float32)
        Wout = jax.random.normal(ks[4], (dim, HIDDEN), dtype=jnp.float32) / np.sqrt(HIDDEN).astype(np.float32)
        bout = jnp.zeros((dim,), dtype=jnp.float32)
        return {'x': x, 'context': context, 'Wq': Wq, 'Wkv': Wkv, 'Wout': Wout, 'bout': bout}
    _L0_xattn_all = _L0_xattn_setup()
    _L0_xattn_in = {k: v for k, v in _L0_xattn_all.items() if k in ('Wq', 'Wkv', 'Wout', 'bout')}
    del _L0_xattn_all

    def _L0_ffn_setup():
        import jax, jax.numpy as jnp
        import numpy as np
        E, K = (16, 4)
        C, H = (256, 448)
        B, T = (2, 64)
        STD = 0.02
        key = jax.random.key(seed)
        ks = jax.random.split(key, 5)
        x = jax.random.normal(ks[0], (B, T, C), jnp.float32)
        W_up = jax.random.normal(ks[1], (E, H, C), jnp.float32) * STD
        W_gate = jax.random.normal(ks[2], (E, H, C), jnp.float32) * STD
        W_down = jax.random.normal(ks[3], (E, C, H), jnp.float32) * STD
        gate_inp = jax.random.normal(ks[4], (E, C), jnp.float32) * STD
        return {'x': x, 'W_up': W_up, 'W_gate': W_gate, 'W_down': W_down, 'gate_inp': gate_inp}
    _L0_ffn_all = _L0_ffn_setup()
    _L0_ffn_in = {k: v for k, v in _L0_ffn_all.items() if k in ('W_up', 'W_gate', 'W_down', 'gate_inp')}
    del _L0_ffn_all

    def _L1_xattn_setup():
        import jax, jax.numpy as jnp
        import numpy as np
        B, Lq, Lk = (2, 512, 128)
        Q_DIM, KV_DIM = (256, 256)
        H, HD = (16, 128)
        KVC, QC, R = (64, 96, 64)
        LOOKBACK = 8
        NEG = -1e+30

        def _rope(x, L):
            half = x.shape[-1] // 2
            inv_freq = 1.0 / 10000.0 ** (jnp.arange(half, dtype=jnp.float32) / half)
            ang = jnp.arange(L, dtype=jnp.float32)[:, None] * inv_freq
            cos, sin = (jnp.cos(ang), jnp.sin(ang))
            x1, x2 = (x[..., :half], x[..., half:])
            return jnp.concatenate([x1 * cos - x2 * sin, x1 * sin + x2 * cos], axis=-1)
        key = jax.random.key(seed)
        ks = jax.random.split(key, 11)

        def w(k, shape, fan_in):
            return jax.random.normal(k, shape, jnp.float32) / np.sqrt(fan_in).astype(np.float32)
        return {'q': jax.random.normal(ks[0], (B, Lq, Q_DIM), jnp.float32), 'kv': jax.random.normal(ks[1], (B, Lk, KV_DIM), jnp.float32), 'seg_id': jnp.sort(jax.random.randint(ks[2], (B, Lq), 0, Lk), axis=-1), 'W_kvc': w(ks[3], (KV_DIM, KVC), KV_DIM), 'W_dq': w(ks[4], (Q_DIM, QC), Q_DIM), 'W_uq': w(ks[5], (QC, H * HD), QC), 'W_qr': w(ks[6], (QC, H * R), QC), 'W_uk': w(ks[7], (KVC, H * HD), KVC), 'W_kr': w(ks[8], (KVC, R), KVC), 'W_uv': w(ks[9], (KVC, H * HD), KVC), 'W_o': w(ks[10], (H * HD, Q_DIM), H * HD)}
    _L1_xattn_all = _L1_xattn_setup()
    _L1_xattn_in = {k: v for k, v in _L1_xattn_all.items() if k in ('W_kvc', 'W_dq', 'W_uq', 'W_qr', 'W_uk', 'W_kr', 'W_uv', 'W_o')}
    del _L1_xattn_all

    def _L1_ffn_setup():
        import jax, jax.numpy as jnp
        import numpy as np
        SWIGLU_ALPHA = 1.702
        SWIGLU_LIMIT = 7.0
        B, S, H, E, K, I = (2, 256, 256, 32, 4, 128)
        key = jax.random.key(seed)
        ks = jax.random.split(key, 8)
        return {'hidden_states': jax.random.normal(ks[0], (B, S, H), jnp.float32), 'gate_w': jax.random.normal(ks[1], (E, H), jnp.float32) * 0.02, 'gate_b': jnp.zeros((E,), jnp.float32), 'w_gate': jax.random.normal(ks[2], (E, H, I), jnp.float32) * 0.02, 'b_gate': jnp.zeros((E, I), jnp.float32), 'w_up': jax.random.normal(ks[3], (E, H, I), jnp.float32) * 0.02, 'b_up': jnp.zeros((E, I), jnp.float32), 'w_down': jax.random.normal(ks[4], (E, I, H), jnp.float32) * 0.02, 'b_down': jnp.zeros((E, H), jnp.float32)}
    _L1_ffn_all = _L1_ffn_setup()
    _L1_ffn_in = {k: v for k, v in _L1_ffn_all.items() if k in ('gate_w', 'gate_b', 'w_gate', 'b_gate', 'w_up', 'b_up', 'w_down', 'b_down')}
    del _L1_ffn_all

    def _L2_xattn_setup():
        import jax, jax.numpy as jnp
        import numpy as np
        key = jax.random.key(seed)
        k1, k2, k3 = jax.random.split(key, 3)
        B, S, D, M = (8, 256, 256, 128)
        hidden_states = jax.random.normal(k1, (B, S, D), dtype=jnp.float32)
        memory_tokens = jax.random.normal(k2, (B, M, D), dtype=jnp.float32)
        memory_mask = jax.random.randint(k3, (B, M), 0, 2).astype(jnp.bool_)
        return {'hidden_states': hidden_states, 'memory_tokens': memory_tokens, 'memory_mask': memory_mask}
    _L2_xattn_all = _L2_xattn_setup()
    _L2_xattn_in = {k: v for k, v in _L2_xattn_all.items() if k in ()}
    del _L2_xattn_all

    def _L2_ffn_setup():
        import jax, jax.numpy as jnp
        import numpy as np
        B, S, H = (2, 256, 256)
        INTER = 128
        N_ROUTED = 8
        ZERO = 4
        TOTAL = N_ROUTED + ZERO
        TOP_K = 2
        SCALE = 1.5
        key = jax.random.key(seed)
        k0, k1, k2, k3, k4, k5 = jax.random.split(key, 6)
        w = 0.02
        return {'hidden_states': jax.random.normal(k0, (B, S, H), jnp.float32), 'classifier_w': jax.random.normal(k1, (TOTAL, H), jnp.float32) * w, 'e_score_correction_bias': jax.random.normal(k2, (TOTAL,), jnp.float32) * w, 'gate_w': jax.random.normal(k3, (N_ROUTED, INTER, H), jnp.float32) * w, 'up_w': jax.random.normal(k4, (N_ROUTED, INTER, H), jnp.float32) * w, 'down_w': jax.random.normal(k5, (N_ROUTED, H, INTER), jnp.float32) * w}
    _L2_ffn_all = _L2_ffn_setup()
    _L2_ffn_in = {k: v for k, v in _L2_ffn_all.items() if k in ('classifier_w', 'e_score_correction_bias', 'gate_w', 'up_w', 'down_w')}
    del _L2_ffn_all

    def _L3_xattn_setup():
        import jax, jax.numpy as jnp
        import numpy as np
        FP8_MAX = 448.0
        EPS = 1e-05

        def _fp8_roundtrip(x):
            return x.astype(jnp.float8_e4m3fn).astype(jnp.float32)

        def _div_clamp_fp8(x, scale):
            y = jnp.clip(x.astype(jnp.float32) / scale, -FP8_MAX, FP8_MAX)
            y = y.astype(jnp.bfloat16).astype(jnp.float32)
            return _fp8_roundtrip(y)

        def _ln(x, w, b):
            mu = jnp.mean(x, axis=-1, keepdims=True)
            var = jnp.mean(jnp.square(x - mu), axis=-1, keepdims=True)
            return (x - mu) * jax.lax.rsqrt(var + EPS) * w + b

        def _fp8_linear_pertensor(x, wq, w_scale, in_scale):
            xq = _div_clamp_fp8(x, in_scale)
            return jnp.einsum('bsi,oi->bso', xq * in_scale, wq) * w_scale

        def _gqa(q, k, v):
            scale = 1.0 / np.sqrt(q.shape[-1])
            scores = jnp.einsum('bsghd,btgd->bghst', q, k) * scale
            p = jax.nn.softmax(scores, axis=-1)
            return jnp.einsum('bghst,btgd->bsghd', p, v)
        key = jax.random.key(seed)
        ks = jax.random.split(key, 8)
        B, S, SC, H, NH, G, D = (2, 256, 64, 256, 16, 8, 128)

        def qw(k, out_f, in_f):
            w = jax.random.normal(k, (out_f, in_f), jnp.float32) * 0.02
            sc = jnp.max(jnp.abs(w)) / FP8_MAX
            return (_fp8_roundtrip(w / sc), sc.astype(jnp.float32))
        wq, wq_s = qw(ks[0], NH * D, H)
        wqx, wqx_s = qw(ks[1], NH * D, H)
        wk, wk_s = qw(ks[2], G * D, H)
        wv, wv_s = qw(ks[3], G * D, H)
        wproj, wp_s = qw(ks[4], H, 2 * NH * D)
        return {'hidden_states': jax.random.normal(ks[5], (B, S, H), jnp.float32), 'cond': jax.random.normal(ks[6], (B, SC, H), jnp.float32), 'ln_w': jnp.ones((H,), jnp.float32), 'ln_b': jnp.zeros((H,), jnp.float32), 'wq': wq, 'wq_scale': wq_s, 'q_in_scale': jnp.full((H,), 0.05, jnp.float32), 'wqx': wqx, 'wqx_scale': wqx_s, 'qx_in_scale': jnp.full((H,), 0.05, jnp.float32), 'wk': wk, 'wk_scale': wk_s, 'k_in_scale': jnp.full((H,), 0.05, jnp.float32), 'wv': wv, 'wv_scale': wv_s, 'v_in_scale': jnp.full((H,), 0.05, jnp.float32), 'w_kv_x': jax.random.normal(ks[7], (2 * G * D, H), jnp.float32) * 0.02, 'qln_w': jnp.ones((D,), jnp.float32), 'qln_b': jnp.zeros((D,), jnp.float32), 'kln_w': jnp.ones((D,), jnp.float32), 'kln_b': jnp.zeros((D,), jnp.float32), 'qxln_w': jnp.ones((D,), jnp.float32), 'qxln_b': jnp.zeros((D,), jnp.float32), 'kxln_w': jnp.ones((D,), jnp.float32), 'kxln_b': jnp.zeros((D,), jnp.float32), 'wproj': wproj, 'proj_w_scale': wp_s, 'proj_in_scale': jnp.asarray(0.05, jnp.float32), 'proj_smooth': jnp.full((2 * NH * D,), 0.05, jnp.float32)}
    _L3_xattn_all = _L3_xattn_setup()
    _L3_xattn_in = {k: v for k, v in _L3_xattn_all.items() if k in ('ln_w', 'ln_b', 'wq', 'wq_scale', 'q_in_scale', 'wqx', 'wqx_scale', 'qx_in_scale', 'wk', 'wk_scale', 'k_in_scale', 'wv', 'wv_scale', 'v_in_scale', 'w_kv_x', 'qln_w', 'qln_b', 'kln_w', 'kln_b', 'qxln_w', 'qxln_b', 'kxln_w', 'kxln_b', 'wproj', 'proj_w_scale', 'proj_in_scale', 'proj_smooth')}
    del _L3_xattn_all

    def _L3_ffn_setup():
        import jax, jax.numpy as jnp
        import numpy as np

        def _sparsify_2to4(h):
            B, S, I = h.shape
            g = h.reshape(B, S, I // 4, 4)
            a = jnp.abs(g)
            _, idx = jax.lax.top_k(a, 2)
            pos = jnp.arange(4)
            mask = (pos == idx[..., 0:1]) | (pos == idx[..., 1:2])
            return (g * mask.astype(g.dtype)).reshape(B, S, I)
        key = jax.random.key(seed)
        k1, k2, k3, k4 = jax.random.split(key, 4)
        B, S, H, I = (4, 256, 256, 1024)
        x = jax.random.normal(k1, (B, S, H), dtype=jnp.float32)
        w_gate = jax.random.normal(k2, (H, I), dtype=jnp.float32) / np.sqrt(H)
        w_up = jax.random.normal(k3, (H, I), dtype=jnp.float32) / np.sqrt(H)
        w_down = jax.random.normal(k4, (I, H), dtype=jnp.float32) / np.sqrt(I)
        return {'x': x, 'w_gate': w_gate, 'w_up': w_up, 'w_down': w_down}
    _L3_ffn_all = _L3_ffn_setup()
    _L3_ffn_in = {k: v for k, v in _L3_ffn_all.items() if k in ('w_gate', 'w_up', 'w_down')}
    del _L3_ffn_all
    return {'x': x, 'ctx_2048': ctx_2048, 'itok_BxS_0_1023': itok_BxS_0_1023, 'mask_BxS2_bk0': mask_BxS2_bk0, 'g_xattn': g_xattn, 'g_ffn': g_ffn, 'L0_xattn_Wq': _L0_xattn_in['Wq'], 'L0_xattn_Wkv': _L0_xattn_in['Wkv'], 'L0_xattn_Wout': _L0_xattn_in['Wout'], 'L0_xattn_bout': _L0_xattn_in['bout'], 'L0_ffn_W_up': _L0_ffn_in['W_up'], 'L0_ffn_W_gate': _L0_ffn_in['W_gate'], 'L0_ffn_W_down': _L0_ffn_in['W_down'], 'L0_ffn_gate_inp': _L0_ffn_in['gate_inp'], 'L1_xattn_W_kvc': _L1_xattn_in['W_kvc'], 'L1_xattn_W_dq': _L1_xattn_in['W_dq'], 'L1_xattn_W_uq': _L1_xattn_in['W_uq'], 'L1_xattn_W_qr': _L1_xattn_in['W_qr'], 'L1_xattn_W_uk': _L1_xattn_in['W_uk'], 'L1_xattn_W_kr': _L1_xattn_in['W_kr'], 'L1_xattn_W_uv': _L1_xattn_in['W_uv'], 'L1_xattn_W_o': _L1_xattn_in['W_o'], 'L1_ffn_gate_w': _L1_ffn_in['gate_w'], 'L1_ffn_gate_b': _L1_ffn_in['gate_b'], 'L1_ffn_w_gate': _L1_ffn_in['w_gate'], 'L1_ffn_b_gate': _L1_ffn_in['b_gate'], 'L1_ffn_w_up': _L1_ffn_in['w_up'], 'L1_ffn_b_up': _L1_ffn_in['b_up'], 'L1_ffn_w_down': _L1_ffn_in['w_down'], 'L1_ffn_b_down': _L1_ffn_in['b_down'], 'L2_ffn_classifier_w': _L2_ffn_in['classifier_w'], 'L2_ffn_e_score_correction_bias': _L2_ffn_in['e_score_correction_bias'], 'L2_ffn_gate_w': _L2_ffn_in['gate_w'], 'L2_ffn_up_w': _L2_ffn_in['up_w'], 'L2_ffn_down_w': _L2_ffn_in['down_w'], 'L3_xattn_ln_w': _L3_xattn_in['ln_w'], 'L3_xattn_ln_b': _L3_xattn_in['ln_b'], 'L3_xattn_wq': _L3_xattn_in['wq'], 'L3_xattn_wq_scale': _L3_xattn_in['wq_scale'], 'L3_xattn_q_in_scale': _L3_xattn_in['q_in_scale'], 'L3_xattn_wqx': _L3_xattn_in['wqx'], 'L3_xattn_wqx_scale': _L3_xattn_in['wqx_scale'], 'L3_xattn_qx_in_scale': _L3_xattn_in['qx_in_scale'], 'L3_xattn_wk': _L3_xattn_in['wk'], 'L3_xattn_wk_scale': _L3_xattn_in['wk_scale'], 'L3_xattn_k_in_scale': _L3_xattn_in['k_in_scale'], 'L3_xattn_wv': _L3_xattn_in['wv'], 'L3_xattn_wv_scale': _L3_xattn_in['wv_scale'], 'L3_xattn_v_in_scale': _L3_xattn_in['v_in_scale'], 'L3_xattn_w_kv_x': _L3_xattn_in['w_kv_x'], 'L3_xattn_qln_w': _L3_xattn_in['qln_w'], 'L3_xattn_qln_b': _L3_xattn_in['qln_b'], 'L3_xattn_kln_w': _L3_xattn_in['kln_w'], 'L3_xattn_kln_b': _L3_xattn_in['kln_b'], 'L3_xattn_qxln_w': _L3_xattn_in['qxln_w'], 'L3_xattn_qxln_b': _L3_xattn_in['qxln_b'], 'L3_xattn_kxln_w': _L3_xattn_in['kxln_w'], 'L3_xattn_kxln_b': _L3_xattn_in['kxln_b'], 'L3_xattn_wproj': _L3_xattn_in['wproj'], 'L3_xattn_proj_w_scale': _L3_xattn_in['proj_w_scale'], 'L3_xattn_proj_in_scale': _L3_xattn_in['proj_in_scale'], 'L3_xattn_proj_smooth': _L3_xattn_in['proj_smooth'], 'L3_ffn_w_gate': _L3_ffn_in['w_gate'], 'L3_ffn_w_up': _L3_ffn_in['w_up'], 'L3_ffn_w_down': _L3_ffn_in['w_down']}

def reference(x, ctx_2048, itok_BxS_0_1023, mask_BxS2_bk0, g_xattn, g_ffn, L0_xattn_Wq, L0_xattn_Wkv, L0_xattn_Wout, L0_xattn_bout, L0_ffn_W_up, L0_ffn_W_gate, L0_ffn_W_down, L0_ffn_gate_inp, L1_xattn_W_kvc, L1_xattn_W_dq, L1_xattn_W_uq, L1_xattn_W_qr, L1_xattn_W_uk, L1_xattn_W_kr, L1_xattn_W_uv, L1_xattn_W_o, L1_ffn_gate_w, L1_ffn_gate_b, L1_ffn_w_gate, L1_ffn_b_gate, L1_ffn_w_up, L1_ffn_b_up, L1_ffn_w_down, L1_ffn_b_down, L2_ffn_classifier_w, L2_ffn_e_score_correction_bias, L2_ffn_gate_w, L2_ffn_up_w, L2_ffn_down_w, L3_xattn_ln_w, L3_xattn_ln_b, L3_xattn_wq, L3_xattn_wq_scale, L3_xattn_q_in_scale, L3_xattn_wqx, L3_xattn_wqx_scale, L3_xattn_qx_in_scale, L3_xattn_wk, L3_xattn_wk_scale, L3_xattn_k_in_scale, L3_xattn_wv, L3_xattn_wv_scale, L3_xattn_v_in_scale, L3_xattn_w_kv_x, L3_xattn_qln_w, L3_xattn_qln_b, L3_xattn_kln_w, L3_xattn_kln_b, L3_xattn_qxln_w, L3_xattn_qxln_b, L3_xattn_kxln_w, L3_xattn_kxln_b, L3_xattn_wproj, L3_xattn_proj_w_scale, L3_xattn_proj_in_scale, L3_xattn_proj_smooth, L3_ffn_w_gate, L3_ffn_w_up, L3_ffn_w_down):
    import jax
    import jax.numpy as jnp

    def _L0_xattn_ref(x, context, Wq, Wkv, Wout, bout):
        import jax, jax.numpy as jnp
        import numpy as np
        HEADS = 8
        DIM_HEAD = 64
        HIDDEN = HEADS * DIM_HEAD
        b = x.shape[0]
        q = jnp.einsum('oc,bcn->bon', Wq, x)
        kv = jnp.einsum('oc,bcm->bom', Wkv, context)
        k, v = jnp.split(kv, 2, axis=1)
        split_heads = lambda t: t.reshape(b, HEADS, DIM_HEAD, t.shape[-1])
        q, k, v = (split_heads(q), split_heads(k), split_heads(v))
        sim = jnp.einsum('bhdi,bhdj->bhij', q, k)
        attn = jax.nn.softmax(sim, axis=-1)
        out = jnp.einsum('bhij,bhdj->bhid', attn, v)
        out = jnp.transpose(out, (0, 1, 3, 2)).reshape(b, HIDDEN, -1)
        return jnp.einsum('oc,bcn->bon', Wout, out) + bout[None, :, None]

    def _L0_ffn_ref(x, W_up, W_gate, W_down, gate_inp):
        import jax, jax.numpy as jnp
        import numpy as np
        E, K = (16, 4)
        C, H = (256, 448)
        B, T = (2, 64)
        STD = 0.02
        b, t, c = x.shape
        xf = x.reshape(b * t, c)
        logits = xf @ gate_inp.T
        topv, topi = jax.lax.top_k(logits, K)
        w = jax.nn.softmax(topv.astype(jnp.float32), axis=-1).astype(x.dtype)
        n = xf.shape[0]
        dense_w = jnp.zeros((n, E), x.dtype).at[jnp.arange(n)[:, None], topi].set(w)
        u = jnp.einsum('nc,ehc->neh', xf, W_up)
        g = jnp.einsum('nc,ehc->neh', xf, W_gate)
        h = jax.nn.silu(g) * u
        y = jnp.einsum('neh,ech,ne->nc', h, W_down, dense_w)
        return y.reshape(b, t, c)

    def _L1_xattn_ref(q, kv, seg_id, W_kvc, W_dq, W_uq, W_qr, W_uk, W_kr, W_uv, W_o):
        import jax, jax.numpy as jnp
        import numpy as np
        B, Lq, Lk = (2, 512, 128)
        Q_DIM, KV_DIM = (256, 256)
        H, HD = (16, 128)
        KVC, QC, R = (64, 96, 64)
        LOOKBACK = 8
        NEG = -1e+30

        def _rope(x, L):
            half = x.shape[-1] // 2
            inv_freq = 1.0 / 10000.0 ** (jnp.arange(half, dtype=jnp.float32) / half)
            ang = jnp.arange(L, dtype=jnp.float32)[:, None] * inv_freq
            cos, sin = (jnp.cos(ang), jnp.sin(ang))
            x1, x2 = (x[..., :half], x[..., half:])
            return jnp.concatenate([x1 * cos - x2 * sin, x1 * sin + x2 * cos], axis=-1)
        b, lq, _ = q.shape
        lk = kv.shape[1]
        kv_c = kv @ W_kvc
        q_c = q @ W_dq
        q_nope = (q_c @ W_uq).reshape(b, lq, H, HD).transpose(0, 2, 1, 3)
        q_rope = (q_c @ W_qr).reshape(b, lq, H, R).transpose(0, 2, 1, 3)
        k_nope = (kv_c @ W_uk).reshape(b, lk, H, HD)
        v = (kv_c @ W_uv).reshape(b, lk, H, HD)
        k_rope = kv_c @ W_kr
        q_rope = _rope(q_rope, lq)
        k_rope = _rope(k_rope, lk)
        scale = 1.0 / np.sqrt(HD + R).astype(np.float32)
        scores = (jnp.einsum('bhqd,bkhd->bhqk', q_nope, k_nope) + jnp.einsum('bhqr,bkr->bhqk', q_rope, k_rope)) * scale
        k_ids = jnp.arange(lk)[None, None, :]
        qs = seg_id[:, :, None]
        good = (k_ids <= qs) & (k_ids >= qs - LOOKBACK)
        scores = jnp.where(good[:, None, :, :], scores, NEG)
        attn = jax.nn.softmax(scores, axis=-1)
        out = jnp.einsum('bhqk,bkhd->bqhd', attn, v).reshape(b, lq, H * HD)
        return out @ W_o

    def _L1_ffn_ref(hidden_states, gate_w, gate_b, w_gate, b_gate, w_up, b_up, w_down, b_down):
        import jax, jax.numpy as jnp
        import numpy as np
        SWIGLU_ALPHA = 1.702
        SWIGLU_LIMIT = 7.0
        B, S, H, E, K, I = (2, 256, 256, 32, 4, 128)
        Bb, Ss, Hh = hidden_states.shape
        x = hidden_states.reshape(-1, Hh)
        logits = x @ gate_w.T + gate_b
        topk_logits, topk_idx = jax.lax.top_k(logits, K)
        topk_weight = jax.nn.softmax(topk_logits.astype(jnp.float32), axis=-1)
        flat_idx = topk_idx.reshape(-1)
        xs = jnp.repeat(x, K, axis=0)
        order = jnp.argsort(flat_idx)
        xt = xs[order]
        gid = flat_idx[order]
        group_sizes = jnp.bincount(flat_idx, length=E).astype(jnp.int32)
        gate = jax.lax.ragged_dot(xt, w_gate, group_sizes) + b_gate[gid]
        up = jax.lax.ragged_dot(xt, w_up, group_sizes) + b_up[gid]
        gate = jnp.minimum(gate, SWIGLU_LIMIT)
        up = jnp.clip(up, -SWIGLU_LIMIT, SWIGLU_LIMIT)
        glu = gate * jax.nn.sigmoid(SWIGLU_ALPHA * gate)
        activated = (up + 1.0) * glu
        outs = jax.lax.ragged_dot(activated, w_down, group_sizes) + b_down[gid]
        inv = jnp.argsort(order)
        outs = outs[inv].reshape(-1, K, Hh)
        y = jnp.sum(outs * topk_weight[..., None], axis=1).astype(x.dtype)
        return y.reshape(Bb, Ss, Hh)

    def _L2_xattn_ref(hidden_states, memory_tokens, memory_mask):
        import jax, jax.numpy as jnp
        import numpy as np
        B, S, D = hidden_states.shape
        scale = 1.0 / jnp.sqrt(jnp.asarray(D, hidden_states.dtype))
        scores = jnp.einsum('bsd,bmd->bsm', hidden_states, memory_tokens) * scale
        neg_inf = jnp.asarray(-1e+30, scores.dtype)
        scores = jnp.where(memory_mask[:, None, :], scores, neg_inf)
        attn = jax.nn.softmax(scores, axis=-1)
        readout = jnp.einsum('bsm,bmd->bsd', attn, memory_tokens)
        valid_b = jnp.any(memory_mask, axis=-1)
        out = jnp.where(valid_b[:, None, None], readout, jnp.zeros_like(readout))
        return out

    def _L2_ffn_ref(hidden_states, classifier_w, e_score_correction_bias, gate_w, up_w, down_w):
        import jax, jax.numpy as jnp
        import numpy as np
        B, S, H = (2, 256, 256)
        INTER = 128
        N_ROUTED = 8
        ZERO = 4
        TOTAL = N_ROUTED + ZERO
        TOP_K = 2
        SCALE = 1.5
        x = hidden_states
        total = classifier_w.shape[0]
        n_routed = gate_w.shape[0]
        logits = jnp.einsum('bsh,eh->bse', x, classifier_w)
        probs = jax.nn.softmax(logits, axis=-1)
        biased = probs + e_score_correction_bias
        _, idx = jax.lax.top_k(biased, TOP_K)
        rw = jnp.take_along_axis(probs, idx, axis=-1) * SCALE
        w_full = jnp.sum(jax.nn.one_hot(idx, total, dtype=x.dtype) * rw[..., None], axis=-2)
        g = jnp.einsum('bsh,eih->bsei', x, gate_w)
        u = jnp.einsum('bsh,eih->bsei', x, up_w)
        act = jax.nn.silu(g) * u
        expert_out = jnp.einsum('bsei,ehi->bseh', act, down_w)
        out = jnp.einsum('bse,bseh->bsh', w_full[..., :n_routed], expert_out)
        out = out + x * jnp.sum(w_full[..., n_routed:], axis=-1, keepdims=True)
        return out

    def _L3_xattn_ref(hidden_states, cond, ln_w, ln_b, wq, wq_scale, q_in_scale, wqx, wqx_scale, qx_in_scale, wk, wk_scale, k_in_scale, wv, wv_scale, v_in_scale, w_kv_x, qln_w, qln_b, kln_w, kln_b, qxln_w, qxln_b, kxln_w, kxln_b, wproj, proj_w_scale, proj_in_scale, proj_smooth):
        import jax, jax.numpy as jnp
        import numpy as np
        FP8_MAX = 448.0
        EPS = 1e-05

        def _fp8_roundtrip(x):
            return x.astype(jnp.float8_e4m3fn).astype(jnp.float32)

        def _div_clamp_fp8(x, scale):
            y = jnp.clip(x.astype(jnp.float32) / scale, -FP8_MAX, FP8_MAX)
            y = y.astype(jnp.bfloat16).astype(jnp.float32)
            return _fp8_roundtrip(y)

        def _ln(x, w, b):
            mu = jnp.mean(x, axis=-1, keepdims=True)
            var = jnp.mean(jnp.square(x - mu), axis=-1, keepdims=True)
            return (x - mu) * jax.lax.rsqrt(var + EPS) * w + b

        def _fp8_linear_pertensor(x, wq, w_scale, in_scale):
            xq = _div_clamp_fp8(x, in_scale)
            return jnp.einsum('bsi,oi->bso', xq * in_scale, wq) * w_scale

        def _gqa(q, k, v):
            scale = 1.0 / np.sqrt(q.shape[-1])
            scores = jnp.einsum('bsghd,btgd->bghst', q, k) * scale
            p = jax.nn.softmax(scores, axis=-1)
            return jnp.einsum('bghst,btgd->bsghd', p, v)
        b, s, _ = hidden_states.shape
        sc = cond.shape[1]
        d = qln_w.shape[0]
        nh = wq.shape[0] // d
        g = wk.shape[0] // d
        hpg = nh // g
        ln_out = _ln(hidden_states, ln_w, ln_b)
        q = _fp8_linear_pertensor(ln_out, wq, wq_scale, q_in_scale).reshape(b, s, g, hpg, d)
        q = _ln(q, qln_w, qln_b)
        k = _fp8_linear_pertensor(ln_out, wk, wk_scale, k_in_scale).reshape(b, s, g, d)
        k = _ln(k, kln_w, kln_b)
        v = _fp8_linear_pertensor(ln_out, wv, wv_scale, v_in_scale).reshape(b, s, g, d)
        core = _gqa(q, k, v).reshape(b, s, nh * d)
        qx = _fp8_linear_pertensor(ln_out, wqx, wqx_scale, qx_in_scale).reshape(b, s, g, hpg, d)
        qx = _ln(qx, qxln_w, qxln_b)
        kvx = jnp.einsum('bsi,oi->bso', cond, w_kv_x)
        kx, vx = jnp.split(kvx, 2, axis=-1)
        kx = _ln(kx.reshape(b, sc, g, d), kxln_w, kxln_b)
        vx = vx.reshape(b, sc, g, d)
        xout = _gqa(qx, kx, vx).reshape(b, s, nh * d)
        cat = jnp.concatenate([core, xout], axis=-1)
        catq = _div_clamp_fp8(cat, proj_smooth)
        return jnp.einsum('bsi,oi->bso', catq, wproj) * (proj_in_scale * proj_w_scale)

    def _L3_ffn_ref(x, w_gate, w_up, w_down):
        import jax, jax.numpy as jnp
        import numpy as np

        def _sparsify_2to4(h):
            B, S, I = h.shape
            g = h.reshape(B, S, I // 4, 4)
            a = jnp.abs(g)
            _, idx = jax.lax.top_k(a, 2)
            pos = jnp.arange(4)
            mask = (pos == idx[..., 0:1]) | (pos == idx[..., 1:2])
            return (g * mask.astype(g.dtype)).reshape(B, S, I)
        h = jax.nn.silu(jnp.einsum('bsh,hi->bsi', x, w_gate)) * jnp.einsum('bsh,hi->bsi', x, w_up)
        h_sparse = _sparsify_2to4(h)
        return jnp.einsum('bsi,ih->bsh', h_sparse, w_down)
    x = x + jnp.tanh(g_xattn[0]) * _L0_xattn_ref(_layernorm(x, axis=-1), ctx_2048, L0_xattn_Wq, L0_xattn_Wkv, L0_xattn_Wout, L0_xattn_bout)
    x = x + jnp.tanh(g_ffn[0]) * _L0_ffn_ref(_layernorm(x, axis=-1), L0_ffn_W_up, L0_ffn_W_gate, L0_ffn_W_down, L0_ffn_gate_inp)
    x = x + jnp.tanh(g_xattn[1]) * _L1_xattn_ref(_layernorm(x, axis=-1), ctx_2048, itok_BxS_0_1023, L1_xattn_W_kvc, L1_xattn_W_dq, L1_xattn_W_uq, L1_xattn_W_qr, L1_xattn_W_uk, L1_xattn_W_kr, L1_xattn_W_uv, L1_xattn_W_o)
    x = x + jnp.tanh(g_ffn[1]) * _L1_ffn_ref(_layernorm(x, axis=-1), L1_ffn_gate_w, L1_ffn_gate_b, L1_ffn_w_gate, L1_ffn_b_gate, L1_ffn_w_up, L1_ffn_b_up, L1_ffn_w_down, L1_ffn_b_down)
    x = x + jnp.tanh(g_xattn[2]) * _L2_xattn_ref(_layernorm(x, axis=-1), ctx_2048, mask_BxS2_bk0)
    x = x + jnp.tanh(g_ffn[2]) * _L2_ffn_ref(_layernorm(x, axis=-1), L2_ffn_classifier_w, L2_ffn_e_score_correction_bias, L2_ffn_gate_w, L2_ffn_up_w, L2_ffn_down_w)
    x = x + jnp.tanh(g_xattn[3]) * _L3_xattn_ref(_layernorm(x, axis=-1), ctx_2048, L3_xattn_ln_w, L3_xattn_ln_b, L3_xattn_wq, L3_xattn_wq_scale, L3_xattn_q_in_scale, L3_xattn_wqx, L3_xattn_wqx_scale, L3_xattn_qx_in_scale, L3_xattn_wk, L3_xattn_wk_scale, L3_xattn_k_in_scale, L3_xattn_wv, L3_xattn_wv_scale, L3_xattn_v_in_scale, L3_xattn_w_kv_x, L3_xattn_qln_w, L3_xattn_qln_b, L3_xattn_kln_w, L3_xattn_kln_b, L3_xattn_qxln_w, L3_xattn_qxln_b, L3_xattn_kxln_w, L3_xattn_kxln_b, L3_xattn_wproj, L3_xattn_proj_w_scale, L3_xattn_proj_in_scale, L3_xattn_proj_smooth)
    x = x + jnp.tanh(g_ffn[3]) * _L3_ffn_ref(_layernorm(x, axis=-1), L3_ffn_w_gate, L3_ffn_w_up, L3_ffn_w_down)
    return x

_drawn_inputs = setup_inputs


def setup_inputs(seed=0):
    import zlib

    import numpy as np

    out = dict(_drawn_inputs(seed))
    spreads = {'L0_xattn_bout': (0.0, 0.34),
     'L1_ffn_gate_b': (0.0, 0.306),
     'L1_ffn_b_gate': (0.0, 0.742),
     'L1_ffn_b_up': (0.0, 0.8),
     'L1_ffn_b_down': (0.0, 0.1),
     'L3_xattn_ln_w': (1.0, 0.552),
     'L3_xattn_ln_b': (0.0, 0.881),
     'L3_xattn_q_in_scale': (0.05000000074505806, 0.6),
     'L3_xattn_qx_in_scale': (0.05000000074505806, 0.6),
     'L3_xattn_k_in_scale': (0.05000000074505806, 0.6),
     'L3_xattn_v_in_scale': (0.05000000074505806, 0.6),
     'L3_xattn_qln_w': (1.0, 0.6),
     'L3_xattn_qln_b': (0.0, 0.8),
     'L3_xattn_kln_w': (1.0, 0.6),
     'L3_xattn_kln_b': (0.0, 2.0),
     'L3_xattn_qxln_w': (1.0, 0.6),
     'L3_xattn_qxln_b': (0.0, 2.0),
     'L3_xattn_kxln_w': (1.0, 0.6),
     'L3_xattn_kxln_b': (0.0, 2.0),
     'L3_xattn_proj_smooth': (0.05000000074505806, 0.6)}
    factors = {'g_ffn': 29.736,
     'L0_ffn_W_up': 5.029,
     'L0_ffn_W_gate': 5.041,
     'L0_ffn_W_down': 5.11,
     'L0_ffn_gate_inp': 5.475,
     'L1_ffn_w_gate': 3.114,
     'L1_ffn_w_up': 6.365,
     'L1_ffn_w_down': 2.927,
     'L2_ffn_gate_w': 8.0,
     'L2_ffn_up_w': 8.0,
     'L2_ffn_down_w': 8.0}
    for name, (base, spread) in spreads.items():
        noise = np.random.default_rng([zlib.crc32(name.encode()), seed]).standard_normal(out[name].shape)
        drawn = base * np.exp(spread * noise) if base else spread * noise
        out[name] = jnp.asarray(drawn.astype(out[name].dtype))
    for name, factor in factors.items():
        out[name] = (out[name] * factor).astype(out[name].dtype)
    return out
```

```python
from contextlib import ExitStack

import concourse.bass as bass
from concourse import mybir

F32 = mybir.dt.float32
BF16 = mybir.dt.bfloat16
I32 = mybir.dt.int32
U32 = mybir.dt.uint32
U8 = mybir.dt.uint8
U16 = mybir.dt.uint16
ALU = mybir.AluOpType
ACT = mybir.ActivationFunctionType
X = mybir.AxisListType.X

P = 128
TOKENS, D = 1024, 256
TILES = TOKENS // P
S = 64
BATCHES = TOKENS // S
EPS = 1e-5
BANK = 512


def repeat(ap, axis, n):
    wide = ap.unsqueeze(axis)
    shape = list(wide.shape)
    shape[axis] = n
    return wide.to_broadcast(shape)


def r32(ap):
    return ap.bitcast(mybir.dt.float32r)


PRODUCTS = ((0, 0), (0, 1), (1, 0))


def tile_of(t, i):
    return t[:, bass.ts(i, 1), :].rearrange("p a n -> p (a n)")


class Steps:

    def __init__(self, eng, sem):
        self.eng, self.sem, self.n, self.turn = eng, sem, 0, 0

    def link(self, ins):
        ins.then_inc(self.sem, 1)
        self.n += 1
        self.eng.wait_ge(self.sem, self.turn + self.n)

    def loop(self, i, per_turn):
        self.turn, self.first, self.per_turn = i * per_turn, self.n, per_turn

    def end(self, turns):
        assert self.n == self.first + self.per_turn, (self.n - self.first)
        self.n, self.turn = self.first + turns * self.per_turn, 0


class Counter:

    def __init__(self, sem, base):
        self.sem, self.base = sem, base


class Kit:

    def __init__(self, nc, ctx, ins, out):
        self.nc, self.ctx, self.ins, self.out = nc, ctx, ins, out
        self.top, self.shared = 0, {}
        self.psum = ctx.enter_context(nc.psum_tensor("psum", [P, 8, BANK], F32))

    def sb(self, name, shape, dt=F32):
        return self.ctx.enter_context(self.nc.sbuf_tensor(name, shape, dt))

    def local(self, name, shape, dt=F32):
        size = 4 if dt in (F32, I32, U32) else 2 if dt == BF16 else 1
        for n in shape[1:]:
            size *= n
        t = self.nc.alloc_sbuf_tensor_at(name, shape, dt, offset=self.base + self.top)
        self.top += (size + 31) // 32 * 32
        assert self.base + self.top <= 229000, (name, self.base + self.top)
        return t

    def sem(self, name):
        return self.ctx.enter_context(self.nc.semaphore(name))

    def counter(self, name, total):
        if name not in self.shared:
            self.shared[name] = [self.sem(name), 0]
        sem, base = self.shared[name]
        self.shared[name][1] += total
        return Counter(sem, base)

    def bank(self, i, n=BANK):
        return self.psum[:, i, 0:n]

    def banks(self, i, k):
        return self.psum[:, i:i + k, :].rearrange("p k n -> p (k n)")




def norm_stage(k, name, feature_major):
    stats_ready = k.counter("norm_stats_ready", 1)
    root_ready = k.counter("norm_root_ready", 1)
    rows_ready = k.counter("norm_rows_ready", TILES)
    turned = k.counter("norm_turned", TILES if feature_major else 0)
    copied = k.counter("norm_copied", TILES if feature_major else 0)
    x, xn, xnT, psum = k.x, k.xn, k.xnT, k.psum

    def vector(v, st):
        for t in range(TILES):
            ins = v.bn_stats(k.bn[:, t, :], x[:, t, :])
        st.link(ins)
        for t in range(TILES):
            ins = v.bn_aggr(k.mean_var[:, t, :], k.bn[:, t, :])
        st.link(ins)
        v.tensor_scalar(k.var[:, :], k.mean_var[:, :, 1], EPS, None, ALU.add).then_inc(stats_ready.sem, 1)
        v.wait_ge(root_ready.sem, root_ready.base + 1)
        for t in range(TILES):
            v.tensor_scalar(xn[:, t, :], x[:, t, :], k.mean_var[:, t, 0:1], k.rstd[:, t:t + 1],
                            ALU.subtract, ALU.mult).then_inc(rows_ready.sem, 1)
        v.wait_ge(rows_ready.sem, rows_ready.base + TILES)
        if feature_major:
            v.wait_ge(copied.sem, copied.base + TILES)

    def gpsimd(g):
        g.wait_ge(stats_ready.sem, stats_ready.base + 1)
        g.tensor_tensor(k.rstd[:, :], k.var[:, :], k.minus_half[:, :], ALU.pow).then_inc(root_ready.sem, 1)

    def scalar(a):
        if feature_major:
            for t in range(TILES):
                a.wait_ge(turned.sem, turned.base + t + 1)
                a.copy(xnT[:, :, t * P:(t + 1) * P], psum[:, t % 2, 0:2 * P].rearrange("p (h n) -> p h n", h=2)
                       ).then_inc(copied.sem, 1)
            a.wait_ge(copied.sem, copied.base + TILES)

    def tensor(pe):
        pe.wait_ge(rows_ready.sem, rows_ready.base + (1 if feature_major else TILES))
        if feature_major:
            for t in range(TILES):
                pe.wait_ge(rows_ready.sem, rows_ready.base + t + 1)
                if t >= 2:
                    pe.wait_ge(copied.sem, copied.base + t - 1)
                for h in range(2):
                    ins = pe.transpose(psum[:, t % 2, h * P:(h + 1) * P], xn[:, t, h * P:(h + 1) * P], k.ident[:, :])
                ins.then_inc(turned.sem, 1)
            pe.wait_ge(copied.sem, copied.base + TILES)

    return dict(vector=vector, gpsimd=gpsimd, scalar=scalar, tensor=tensor)




def l0_attention(k):
    nc, psum, ins, gate = k.nc, k.psum, k.ins, k.gate
    HEADS, HD = 8, 64
    UNITS = 4 * HEADS
    TURNS, DEPTH = TILES // 2, 8
    k.top = 0
    wq = k.local("l0_wq", [HD, HEADS, P])
    wk = k.local("l0_wk", [HD, HEADS, HD])
    wv = k.local("l0_wv", [HD, HEADS, HD])
    wo = k.local("l0_wo", [HD, HEADS, HD])
    bout = k.local("l0_bout", [P, 1])
    a_pad = k.local("l0_a_pad", [P, 2, HEADS * HD])
    b_t = k.local("l0_b_t", [HD, HEADS * HD])
    ctx2 = k.local("l0_ctx2", [P, 2, 2, 256])
    t_sb = k.local("l0_t", [P, 2, 4, 256])
    u_sb = k.local("l0_u", [P, 2, 2, HEADS, HD + 1])
    probs = k.local("l0_probs", [P, 2, 2, 256])
    probs_t = k.local("l0_probs_t", [P, 2, 2, 256])
    nmax = k.local("l0_nmax", [P, 2, 2])
    rsum = k.local("l0_rsum", [P, 2, 4])
    scaled = k.local("l0_scaled", [P, 2, HEADS, HD])
    out_t = k.local("l0_out_t", [P, 2, 2, P])
    upd = k.local("l0_upd", [P, 256])

    w_in, ctx_in = k.sem("l0_w_in"), [k.sem("l0_ctx_in0"), k.sem("l0_ctx_in1")]
    zeroed, folded, fold_copied = k.sem("l0_zeroed"), k.sem("l0_folded"), k.sem("l0_fold_copied")
    t_done, t_copied = k.sem("l0_t_done"), k.sem("l0_t_copied")
    u_done, u_copied = k.sem("l0_u_done"), k.sem("l0_u_copied")
    sim_ready, nmax_ready, probs_ready = k.sem("l0_sim_ready"), k.sem("l0_nmax_ready"), k.sem("l0_probs_ready")
    turned, turn_copied = k.sem("l0_turned"), k.sem("l0_turn_copied")
    pv_done, half_read = k.sem("l0_pv_done"), k.sem("l0_half_read")
    out_ready, out_turned, x_added = k.sem("l0_out_ready"), k.sem("l0_out_turned"), k.sem("l0_x_added")

    def head(i, g, lag=0):
        return not isinstance(i, int) or 0 <= UNITS * i + g - lag < TURNS * UNITS

    def later(i, g, n):
        return not isinstance(i, int) or UNITS * i + g >= n

    def next_batch(i, g):
        n = g // HEADS + 1
        return n if not isinstance(i, int) or 4 * i + n < 4 * TURNS else None

    def all_stages(eng, stage, loop=lambda i: None, end=lambda: None):
        for g in range(DEPTH):
            stage(0, g)
        with eng.Fori(0, TURNS - 1) as i:
            loop(i)
            for g in range(DEPTH, DEPTH + UNITS):
                stage(i, g)
            end()
        for g in range(DEPTH, DEPTH + UNITS):
            stage(TURNS - 1, g)

    def sync(sp):
        for dst, name in ((wq, "l0_wq"), (wk, "l0_wk"), (wv, "l0_wv"), (wo, "l0_wo"), (bout, "l0_bout")):
            sp.dma_start(dst[:], ins[name]).then_inc(w_in, 16)

        def load_ctx(t, s):
            for b in range(2):
                src = ins["ctx"][bass.ts(t * 2 + b, 1)].rearrange("a s d -> (a s) d")
                for half in range(2):
                    sp.dma_start(ctx2[64 * half:64 * half + 64, s, b, :], src).then_inc(ctx_in[s], 16)

        for s in range(2):
            load_ctx(s, s)
        with sp.Fori(0, TILES // 2 - 1) as i:
            for s in range(2):
                sp.wait_ge(x_added, 2 * i + s + 2)
                load_ctx(2 * i + 2 + s, s)

    def gpsimd(g):
        g.memset(a_pad[:], 0.0).then_inc(zeroed, 1)
        g.memset(u_sb[:], 1.0).then_inc(zeroed, 1)

    def tensor(pe):
        pe.wait_ge(w_in, 5 * 16)
        for h in range(HEADS):
            c = slice(h * HD, (h + 1) * HD)
            pe.matmul(psum[:, 2, c], wq[:, h, :], wk[:, h, :], start=True, stop=True)
            last = pe.matmul(psum[0:HD, 3, c], wv[:, h, :], wo[:, h, :], start=True, stop=True)
        last.then_inc(folded, 1)
        pe.wait_ge(fold_copied, 3)

        def t_of(i, n):
            s, b = n // 2 % 2, n % 2
            if later(i, n * HEADS, 1):
                pe.wait_ge(u_copied, 4 * i + n)
            if b == 0 and later(i, n * HEADS, 1):
                pe.wait_ge(x_added, 2 * i + n // 2)
            for hp in range(4):
                last = pe.matmul(psum[:, 6 + hp // 2, 256 * (hp % 2):256 * (hp % 2) + 256],
                                 a_pad[:, b, hp * P:(hp + 1) * P], tile_of(k.xn, 2 * i + n // 2),
                                 start=True, stop=True)
            last.then_inc(t_done, 1)

        def u_of(i, n):
            s, b = n // 2 % 2, n % 2
            pe.wait_ge(ctx_in[s], 64 * (i + n // 4 + 1))
            pe.wait_ge(t_copied, 4 * i + n + 1)
            for jt in range(2):
                last = pe.matmul(psum[:, 6 + jt, :], ctx2[0:HD, s, b, jt * P:(jt + 1) * P], b_t[:, :],
                                 start=True, stop=True)
            last.then_inc(u_done, 1)

        def sim(i, g):
            n, h = divmod(g, HEADS)
            s, b = n // 2 % 2, n % 2
            if h == 0:
                pe.wait_ge(t_copied, 4 * i + n + 1)
            if later(i, g, 2):
                pe.wait_ge(probs_ready, UNITS * i + g - 1)
            r = slice(64 * (h % 2), 64 * (h % 2) + 64)
            for it in range(2):
                last = pe.matmul(psum[:, g % 2, 256 * it:256 * it + 256],
                                 t_sb[r, n % 2, h // 2, it * P:(it + 1) * P], ctx2[r, s, b, :],
                                 start=True, stop=True)
            last.then_inc(sim_ready, 1)

        def turn(i, g):
            pe.wait_ge(probs_ready, UNITS * i + g + 1)
            if later(i, g, 2):
                pe.wait_ge(turn_copied, UNITS * i + g - 1)
            for jt in range(2):
                for it in range(2):
                    last = pe.transpose(psum[:, 2 + g % 2, 256 * jt + it * P:256 * jt + (it + 1) * P],
                                        probs[:, g % 2, it, jt * P:(jt + 1) * P], k.ident[:, :])
            last.then_inc(turned, 1)

        def pv(i, g):
            n, h = divmod(g, HEADS)
            pe.wait_ge(turn_copied, UNITS * i + g + 1)
            if h == 0:
                pe.wait_ge(u_copied, 4 * i + n + 1)
            if h % 4 == 0 and later(i, g, 1):
                pe.wait_ge(half_read, 8 * i + g // 4)
            for it in range(2):
                for jt in range(2):
                    last = pe.matmul(psum[:, 4 + it, 65 * (h % 4):65 * (h % 4) + 65],
                                     probs_t[:, g % 2, jt, it * P:(it + 1) * P], u_sb[:, n % 2, jt, h, :],
                                     start=(jt == 0), stop=(jt == 1))
            last.then_inc(pv_done, 1)

        def turn_out(i, s, made):
            pe.wait_ge(out_ready, 2 * i + s + 1)
            pe.wait_ge(u_copied, made)
            for it in range(2):
                last = pe.transpose(psum[:, 6, it * P:(it + 1) * P], out_t[:, s, it, :], k.ident[:, :])
            last.then_inc(out_turned, 1)

        def stage(i, g):
            if head(i, g):
                sim(i, g)
            if head(i, g, 1):
                turn(i, g - 1)
            if head(i, g, 2):
                pv(i, g - 2)
            n = next_batch(i, g)
            if g % HEADS == 2 and n is not None:
                t_of(i, n)
            if g % HEADS == 4 and n is not None:
                u_of(i, n)
            if g in (22, 38):
                turn_out(i, g // 38, 4 * i + (g // HEADS + 2 if n is not None else 4))

        t_of(0, 0)
        u_of(0, 0)
        all_stages(pe, stage)

    def vector(v, st):
        v.sem_inc(x_added, 1)

        def normalise(i, half):
            n, hf = divmod(half, 2)
            v.wait_ge(pv_done, UNITS * i + 4 * half + 4)
            pair = psum[:, 4:6, 0:260].rearrange("p k (h o) -> p k h o", h=4)
            st.link(v.reciprocal(rsum[:, :, :], pair[:, :, :, HD]))
            for it in range(2):
                last = v.tensor_tensor(scaled[:, it, 4 * hf:4 * hf + 4, :], pair[:, it, :, 0:HD],
                                       repeat(rsum[:, it, :], 2, HD), ALU.mult)
            last.then_inc(half_read, 1)
            if hf == 1:
                v.wait_ge(half_read, 8 * i + half + 1)
                s, b = n // 2 % 2, n % 2
                for it in range(2):
                    last = v.tensor_reduce(out_t[:, s, it, b * HD:(b + 1) * HD],
                                           scaled[:, it, :, :].rearrange("p h o -> p o h"), X, ALU.add)
                if b == 1:
                    last.then_inc(out_ready, 1)

        def add(i, s):
            v.wait_ge(out_turned, 2 * i + s + 1)
            st.link(v.tensor_scalar(upd[:, :], psum[:, 6, 0:256], bout[:, 0:1], gate, ALU.add, ALU.mult))
            xt = tile_of(k.x, 2 * i + s)
            v.tensor_tensor(xt, xt, upd[:, :], ALU.add).then_inc(x_added, 1)
            v.wait_ge(x_added, 2 * i + s + 2)

        def stage(i, g):
            if head(i, g):
                v.wait_ge(sim_ready, UNITS * i + g + 1)
                if later(i, g, 2):
                    v.wait_ge(probs_ready, UNITS * i + g - 1)
                v.tensor_reduce(nmax[:, g % 2, :], psum[:, g % 2, :].rearrange("p (t j) -> p t j", t=2), X,
                                ALU.max, negate=True).then_inc(nmax_ready, 1)
            if head(i, g, 1):
                v.wait_ge(turned, UNITS * i + g)
                if later(i, g, 3):
                    v.wait_ge(pv_done, UNITS * i + g - 2)
                v.tensor_copy(probs_t[:, (g - 1) % 2, :, :].rearrange("p a n -> p (a n)"),
                              k.bank(2 + (g - 1) % 2)).then_inc(turn_copied, 1)
            if head(i, g, 2) and (g - 2) % 4 == 3:
                normalise(i, (g - 2) // 4)
            if g in (23, 39):
                add(i, g // 39)

        all_stages(v, stage, lambda i: st.loop(i, 8 + 2), lambda: st.end(TURNS - 1))

    def scalar(a):
        a.wait_ge(zeroed, 2)
        a.wait_ge(folded, 1)
        a.copy(a_pad[0:64, 0, :], psum[0:64, 2, :]).then_inc(fold_copied, 1)
        a.copy(a_pad[64:128, 1, :], psum[64:128, 2, :]).then_inc(fold_copied, 1)
        a.copy(b_t[:, :], psum[0:64, 3, :]).then_inc(fold_copied, 1)
        a.preload_act_table(ACT.Exp)

        def t_copy(i, n):
            a.wait_ge(t_done, 4 * i + n + 1)
            a.copy(t_sb[:, n % 2, :, :].rearrange("p a n -> p (a n)"), k.banks(6, 2)).then_inc(t_copied, 1)

        def u_copy(i, n):
            a.wait_ge(u_done, 4 * i + n + 1)
            for jt in range(2):
                last = a.copy(u_sb[:, n % 2, jt, :, 0:HD], psum[:, 6 + jt, :].rearrange("p (h o) -> p h o", h=HEADS))
            last.then_inc(u_copied, 1)

        def stage(i, g):
            if head(i, g):
                a.wait_ge(nmax_ready, UNITS * i + g + 1)
                if later(i, g, 2):
                    a.wait_ge(turned, UNITS * i + g - 1)
                for it in range(2):
                    last = a.activation(probs[:, g % 2, it, :], psum[:, g % 2, 256 * it:256 * it + 256], ACT.Exp,
                                        bias=nmax[:, g % 2, it:it + 1])
                last.then_inc(probs_ready, 1)
            n = next_batch(i, g)
            if g % HEADS == 2 and n is not None:
                t_copy(i, n)
            if g % HEADS == 4 and n is not None:
                u_copy(i, n)

        t_copy(0, 0)
        u_copy(0, 0)
        all_stages(a, stage)

    return dict(sync=sync, gpsimd=gpsimd, tensor=tensor, vector=vector, scalar=scalar)




def top_mask(v, st, k, scores, E, top, buf):
    for t in range(TILES):
        ins = v.max(buf["top8"][:, t, :], scores[:, t, :])
    st.link(ins)
    for t in range(TILES):
        ins = v.max_index(buf["place"][:, t, :], buf["top8"][:, t, :], scores[:, t, :])
    st.link(ins)
    st.link(v.tensor_copy(buf["place_f"][:, :, :], buf["place"][:, :, :]))
    mask, hit = buf["mask"], buf["hit"]
    for j in range(top):
        st.link(v.tensor_tensor(mask[:, :, :] if j == 0 else hit[:, :, :], repeat(k.iota[:, 0:E], 1, TILES),
                                repeat(buf["place_f"][:, :, j], 2, E), ALU.is_equal))
        if j:
            st.link(v.tensor_tensor(mask[:, :, :], mask[:, :, :], hit[:, :, :], ALU.add))


def routed_ffn(k, name, E, H, HT, top, kind):
    nc, psum, ins, gate = k.nc, k.psum, k.ins, k.gate
    LOGITS = {"l0": E, "l1": E, "l2": 12}[kind]
    NU = HT * 2
    k.top = 0
    w_gu = k.local(name + "_w_gu", [P, 2, 2, 2, HT * H])
    w_dn = k.local(name + "_w_dn", [H, 2, HT, D])
    w_gu2 = k.local(name + "_w_gu2", [P, 2, 2, 2, 2, HT * H])
    w_dn2 = k.local(name + "_w_dn2", [H, 2, 2, HT, D])
    xnT2 = k.local(name + "_xnT2", [P, 2, 2, TOKENS])
    hid2 = k.local(name + "_hid2", [H, 2, 2, HT, TOKENS])
    hid = k.local(name + "_hid", [H, 2, 512])
    act_sb = k.local(name + "_act", [H, 2, 512])
    gate_w = k.local(name + "_gate_w", [P, 2, LOGITS])
    logits = k.local(name + "_logits", [P, TILES, LOGITS])
    shifted = k.local(name + "_shifted", [P, TILES, LOGITS])
    buf = dict(top8=k.local(name + "_top8", [P, TILES, 8]), place=k.local(name + "_place", [P, TILES, 8], U32),
               place_f=k.local(name + "_place_f", [P, TILES, 8]), mask=k.local(name + "_mask", [P, TILES, LOGITS]),
               hit=k.local(name + "_hit", [P, TILES, LOGITS]))
    total = k.local(name + "_total", [P, TILES])
    w_all = k.local(name + "_w_all", [P, LOGITS, TILES])
    w_cur = k.local(name + "_w_cur", [P, 2, TILES])
    w_cur_a = k.local(name + "_w_cur_a", [P, 2, TILES])
    weighted = k.local(name + "_weighted", [P, 2, TILES // 2, D])
    if kind == "l1":
        gate_b = k.local(name + "_gate_b", [P, E])
        bias = k.local(name + "_bias", [H, E, 2])
        bias_cur = k.local(name + "_bias_cur", [H, 2, 2])
        b_down = k.local(name + "_b_down", [E, D])
        w_turned = k.local(name + "_w_turned", [E, TOKENS])
        glu_in = k.local(name + "_glu_in", [H, 2, 512])
        glu = k.local(name + "_glu", [H, 512])
        up_sb = k.local(name + "_up", [H, 2, 512])
    if kind == "l2":
        score_b = k.local(name + "_score_b", [P, LOGITS])
        biased = k.local(name + "_biased", [P, TILES, LOGITS])
        passed = k.local(name + "_passed", [P, TILES, D])

    n_small = {"l0": 1, "l1": 4, "l2": 2}[kind]
    small_in = k.counter("ffn_small_in", 16 * n_small)
    w_in = [k.counter(f"ffn_w_in{s}", 16 * (E // 2)) for s in range(2)]
    w_dn_in = [k.counter(f"ffn_w_dn_in{s}", 16 * (E // 2)) for s in range(2)]
    logits_ready, shifted_ready = k.counter("ffn_logits_ready", 1), k.counter("ffn_shifted_ready", 1)
    exp_ready, gu_ready = k.counter("ffn_exp_ready", 1), k.counter("ffn_gu_ready", NU * E)
    act_ready, hid_ready = k.counter("ffn_act_ready", NU * E), k.counter("ffn_hid_ready", NU * E)
    dn_ready, dn_added = k.counter("ffn_dn_ready", 4 * E + 4), k.counter("ffn_dn_added", 2 * E + 2)
    dn_weighted, gp_added = k.counter("ffn_dn_weighted", 2 * E + 2), k.counter("ffn_gp_added", E + 2)
    w_cur_a_ready = k.counter("ffn_w_cur_a_ready", E)
    weights_ready = k.counter("ffn_weights_ready", 1)
    if kind == "l1":
        glu_in_ready, gu_read = k.counter("ffn_glu_in_ready", NU * E), k.counter("ffn_gu_read", NU * E)
        w_turn_ready, w_turn_copied = k.counter("ffn_w_turn_ready", 2), k.counter("ffn_w_turn_copied", 1)
    xn_high, xn_low = k.counter("ffn_xn_high", 2), k.counter("ffn_xn_low", 2)
    gu_high, gu_low = k.counter("ffn_w_gu_high", E), k.counter("ffn_w_gu_low", E)
    w_dn_high, w_dn_low = k.counter("ffn_w_dn_high", E), k.counter("ffn_w_dn_low", E)
    hid_high, hid_low = k.counter("ffn_hid_high", NU * E), k.counter("ffn_hid_low", NU * E)
    small = [(gate_w[:], ins[name + "_gate_w"])]
    if kind == "l1":
        small += [(gate_b[:], ins["l1_gate_b"].partition_broadcast(P)), (bias[:], ins["l1_bias"]),
                  (b_down[:], ins["l1_b_down"])]
    if kind == "l2":
        small += [(score_b[:], ins["l2_score_b"].partition_broadcast(P))]

    def sync(sp):
        for dst, src in small:
            sp.dma_start(dst, src).then_inc(small_in.sem, 16)

        def load_gate_up(e, s):
            sp.dma_start(w_gu[:, s].rearrange("p h g n -> p (h g n)"),
                         ins[name + "_w_gu"][bass.ts(e, 1)].rearrange("e p n -> p (e n)")).then_inc(w_in[s].sem, 16)

        def load_down(e, s):
            sp.dma_start(w_dn[:, s].rearrange("p h n -> p (h n)"),
                         ins[name + "_w_dn"][bass.ts(e, 1)].rearrange("e p n -> p (e n)")).then_inc(w_dn_in[s].sem, 16)

        load_gate_up(0, 0)
        load_gate_up(1, 1)
        load_down(0, 0)
        load_down(1, 1)
        with sp.Fori(0, E // 2 - 1) as i:
            for s in range(2):
                sp.wait_ge(gu_low.sem, gu_low.base + 2 * i + s + 1)
                load_gate_up(2 * i + 2 + s, s)
                sp.wait_ge(w_dn_low.sem, w_dn_low.base + 2 * i + s + 1)
                load_down(2 * i + 2 + s, s)

    banks_read = gu_read if kind == "l1" else hid_ready

    def tensor(pe):
        pe.wait_ge(small_in.sem, small_in.base + 16 * n_small)
        for t in range(TILES):
            for h in range(2):
                last = pe.matmul(psum[:, 4, t * LOGITS:(t + 1) * LOGITS], k.xnT[:, h, t * P:(t + 1) * P], gate_w[:, h, :],
                                 start=(h == 0), stop=(h == 1))
        last.then_inc(logits_ready.sem, 1)

        def gate_up(e, s):
            pe.wait_ge(gu_low.sem, gu_low.base + e + 1)
            for u in range(NU):
                ht, nh = divmod(u, 2)
                if isinstance(e, int) and e == 0 and u < 2:
                    pe.wait_ge(xn_low.sem, xn_low.base + nh + 1)
                if not (isinstance(e, int) and NU * e + u < 2):
                    pe.wait_ge(banks_read.sem, banks_read.base + NU * e + u - 1)
                for g in range(2):
                    for m, (wp, xp, h) in enumerate((a, b, h) for h in range(2) for a, b in PRODUCTS):
                        last = pe.matmul(psum[0:H, 2 * (u % 2) + g, :], r32(w_gu2[:, s, wp, h, g, ht * H:(ht + 1) * H]),
                                         r32(xnT2[:, xp, h, nh * 512:nh * 512 + 512]), start=(m == 0), stop=(m == 5))
                last.then_inc(gu_ready.sem, 1)

        def down(e, s):
            pe.wait_ge(w_dn_low.sem, w_dn_low.base + e + 1)
            pe.wait_ge(hid_low.sem, hid_low.base + NU * e + NU)
            for pair in range(4):
                if pair < 2:
                    pe.wait_ge(dn_added.sem, dn_added.base + 2 * e + pair + 1)
                else:
                    pe.wait_ge(dn_weighted.sem, dn_weighted.base + 2 * e + pair - 1)
                for half in range(2):
                    t = 2 * pair + half
                    for m, (hp, wp, ht) in enumerate((a, b, ht) for ht in range(HT) for a, b in PRODUCTS):
                        last = pe.matmul(psum[:, 4 + pair, D * half:D * half + D],
                                         r32(hid2[:, s, hp, ht, t * P:(t + 1) * P]), r32(w_dn2[:, s, wp, ht, :]),
                                         start=(m == 0), stop=(m == 3 * HT - 1))
                last.then_inc(dn_ready.sem, 1)

        gate_up(0, 0)
        if kind == "l1":
            pe.wait_ge(weights_ready.sem, weights_ready.base + 1)
            for t in range(TILES):
                last = pe.transpose(psum[0:E, 4 + t // 4, (t % 4) * P:(t % 4 + 1) * P], w_all[:, :, t], k.ident[:, :])
            last.then_inc(w_turn_ready.sem, 1)
            pe.wait_ge(w_turn_copied.sem, w_turn_copied.base + 1)
            for t in range(TILES):
                last = pe.matmul(psum[:, 4 + t // 2, D * (t % 2):D * (t % 2) + D], w_turned[:, t * P:(t + 1) * P],
                                 b_down[:, :], start=True, stop=True)
            last.then_inc(w_turn_ready.sem, 1)
        with pe.Fori(0, E // 2 - 1) as i:
            gate_up(2 * i + 1, 1)
            down(2 * i, 0)
            gate_up(2 * i + 2, 0)
            down(2 * i + 1, 1)
        gate_up(E - 1, 1)
        down(E - 2, 0)
        down(E - 1, 1)

    def vector(v, st):
        v.sem_inc(dn_ready.sem, 4)
        flat = psum[:, 4, 0:TILES * LOGITS].rearrange("p (t e) -> p t e", t=TILES)
        v.wait_ge(small_in.sem, small_in.base + 16 * n_small)
        v.wait_ge(logits_ready.sem, logits_ready.base + 1)
        if kind == "l1":
            st.link(v.tensor_tensor(logits[:, :, :], flat, repeat(gate_b[:, :], 1, TILES), ALU.add))
        else:
            st.link(v.tensor_copy(logits[:, :, :], flat))
        if kind == "l2":
            st.link(v.tensor_reduce(total[:, :], logits[:, :, :], X, ALU.max))
            v.tensor_tensor(shifted[:, :, :], logits[:, :, :], repeat(total[:, :], 2, LOGITS), ALU.subtract
                            ).then_inc(shifted_ready.sem, 1)
            v.wait_ge(exp_ready.sem, exp_ready.base + 1)
            st.link(v.tensor_reduce(total[:, :], shifted[:, :, :], X, ALU.add))
            st.link(v.reciprocal(total[:, :], total[:, :]))
            st.link(v.tensor_tensor(shifted[:, :, :], shifted[:, :, :], repeat(total[:, :], 2, LOGITS), ALU.mult))
            st.link(v.tensor_tensor(biased[:, :, :], shifted[:, :, :], repeat(score_b[:, :], 1, TILES), ALU.add))
            top_mask(v, st, k, biased, LOGITS, top, buf)
            st.link(v.tensor_tensor(shifted[:, :, :], shifted[:, :, :], buf["mask"][:, :, :], ALU.mult))
            v.tensor_scalar(w_all[:, :, :].rearrange("p e t -> p t e"), shifted[:, :, :], 1.5, gate,
                            ALU.mult, ALU.mult).then_inc(weights_ready.sem, 1)
            v.wait_ge(weights_ready.sem, weights_ready.base + 1)
            st.link(v.tensor_reduce(total[:, :], w_all[:, E:LOGITS, :].rearrange("p e t -> p t e"), X, ALU.add))
            st.link(v.tensor_tensor(passed[:, :, :], k.xn[:, :, :], repeat(total[:, :], 2, D), ALU.mult))
            st.link(v.tensor_tensor(k.x[:, :, :], k.x[:, :, :], passed[:, :, :], ALU.add))
        else:
            top_mask(v, st, k, logits, LOGITS, top, buf)
            v.tensor_tensor(shifted[:, :, :], logits[:, :, :], repeat(buf["top8"][:, :, 0], 2, LOGITS), ALU.subtract
                            ).then_inc(shifted_ready.sem, 1)
            v.wait_ge(exp_ready.sem, exp_ready.base + 1)
            st.link(v.tensor_tensor(shifted[:, :, :], shifted[:, :, :], buf["mask"][:, :, :], ALU.mult))
            st.link(v.tensor_reduce(total[:, :], shifted[:, :, :], X, ALU.add))
            st.link(v.reciprocal(total[:, :], total[:, :]))
            st.link(v.tensor_scalar(total[:, :], total[:, :], gate, None, ALU.mult))
            v.tensor_tensor(w_all[:, :, :].rearrange("p e t -> p t e"), shifted[:, :, :],
                            repeat(total[:, :], 2, LOGITS), ALU.mult).then_inc(weights_ready.sem, 1)
            v.wait_ge(weights_ready.sem, weights_ready.base + 1)
        if kind == "l1":
            st.link(v.tensor_scalar(bias[:, :, 1], bias[:, :, 1], 1.0, None, ALU.add))
            v.wait_ge(w_turn_ready.sem, w_turn_ready.base + 1)
            v.tensor_copy(w_turned[:, :], psum[0:E, 4:6, :].rearrange("p a n -> p (a n)")).then_inc(w_turn_copied.sem, 1)

        def hidden(e, s):
            if kind == "l1":
                st.link(v.tensor_copy(bias_cur[:, s, :], bias[:, bass.ts(e, 1), :].rearrange("p a b -> p (a b)")))
            for u in range(NU):
                ht, nh = divmod(u, 2)
                dst = hid[:, u % 2, :]
                if not (isinstance(e, int) and NU * e + u < 2):
                    v.wait_ge(hid_low.sem, hid_low.base + NU * e + u - 1)
                g_bank, u_bank = psum[0:H, 2 * (u % 2), :], psum[0:H, 2 * (u % 2) + 1, :]
                if kind == "l1":
                    v.wait_ge(gu_ready.sem, gu_ready.base + NU * e + u + 1)
                    v.tensor_scalar(glu_in[:, u, :], g_bank, bias_cur[:, s, 0:1], 7.0, ALU.add, ALU.min
                                    ).then_inc(glu_in_ready.sem, 1)
                    v.tensor_scalar(up_sb[:, u, :], u_bank, bias_cur[:, s, 1:2], -6.0, ALU.add, ALU.max
                                    ).then_inc(gu_read.sem, 1)
                    v.wait_ge(act_ready.sem, act_ready.base + NU * e + u + 1)
                    st.link(v.tensor_tensor(glu[:, :], glu_in[:, u, :], act_sb[:, u, :], ALU.mult))
                    v.scalar_tensor_tensor(dst, up_sb[:, u, :], 8.0, glu[:, :], ALU.min, ALU.mult).then_inc(hid_ready.sem, 1)
                    v.wait_ge(hid_ready.sem, hid_ready.base + NU * e + u + 1)
                else:
                    v.wait_ge(act_ready.sem, act_ready.base + NU * e + u + 1)
                    v.tensor_tensor(dst, act_sb[:, u % 2, :], u_bank, ALU.mult).then_inc(hid_ready.sem, 1)

        def add(e, s):
            st.link(v.tensor_copy(w_cur[:, s, :], w_all[:, bass.ts(e, 1), :].rearrange("p a t -> p (a t)")))
            for pair in range(2):
                v.wait_ge(dn_ready.sem, dn_ready.base + 4 * e + pair + 5)
                v.wait_ge(dn_added.sem, dn_added.base + 2 * e + pair + 1)
                for half in range(2):
                    t = 2 * pair + half
                    last = v.scalar_tensor_tensor(k.x[:, t, :], psum[:, 4 + pair, D * half:D * half + D],
                                                  w_cur[:, s, t:t + 1], k.x[:, t, :], ALU.mult, ALU.add)
                last.then_inc(dn_added.sem, 1)

        per_turn = 2 + (2 * (1 + NU) if kind == "l1" else 0)
        hidden(0, 0)
        if kind == "l1":
            v.wait_ge(w_turn_ready.sem, w_turn_ready.base + 2)
            flat = k.x[:, :, :].rearrange("p t d -> p (t d)")
            st.link(v.tensor_tensor(flat, flat, k.banks(4, 4), ALU.add))
        v.sem_inc(dn_added.sem, 2)
        v.sem_inc(dn_weighted.sem, 2)
        v.sem_inc(gp_added.sem, 2)
        with v.Fori(0, E // 2 - 1) as i:
            st.loop(i, per_turn)
            hidden(2 * i + 1, 1)
            add(2 * i, 0)
            hidden(2 * i + 2, 0)
            add(2 * i + 1, 1)
            st.end(E // 2 - 1)
        hidden(E - 1, 1)
        add(E - 2, 0)
        add(E - 1, 1)
        v.wait_ge(dn_added.sem, dn_added.base + 2 * E + 2)
        v.wait_ge(gp_added.sem, gp_added.base + E + 2)

    def run(eng, prepare_gate_up, prepare_down, unit, add):
        def expert(e, s, turn):
            for u in range(NU):
                if u == (NU // 2 if HT > 1 else 0) and not (isinstance(e, int) and e == E - 1):
                    prepare_gate_up(e + 1, 1 - s, turn + s)
                if u == 0:
                    prepare_down(e, s, turn)
                unit(e, s, u)

        expert(0, 0, 0)
        with eng.Fori(0, E // 2 - 1) as i:
            expert(2 * i + 1, 1, i)
            add(2 * i, 0)
            expert(2 * i + 2, 0, i + 1)
            add(2 * i + 1, 1)
        expert(E - 1, 1, E // 2 - 1)
        add(E - 2, 0)
        add(E - 1, 1)

    def scalar(a):
        def prepare_gate_up(e, s, turn):
            a.wait_ge(w_in[s].sem, w_in[s].base + 16 * (turn + 1))
            if not (isinstance(e, int) and e < 2):
                a.wait_ge(gu_ready.sem, gu_ready.base + NU * (e - 1))
            a.copy(r32(w_gu2[:, s, 0]), w_gu[:, s]).then_inc(gu_high.sem, 1)

        def prepare_down(e, s, turn):
            a.wait_ge(w_dn_in[s].sem, w_dn_in[s].base + 16 * (turn + 1))
            if not (isinstance(e, int) and e == 0):
                a.wait_ge(dn_ready.sem, dn_ready.base + 4 * e)
            a.copy(r32(w_dn2[:, s, 0]), w_dn[:, s]).then_inc(w_dn_high.sem, 1)

        def unit(e, s, u):
            ht, nh = divmod(u, 2)
            if kind == "l1":
                a.wait_ge(glu_in_ready.sem, glu_in_ready.base + NU * e + u + 1)
                a.activation(act_sb[:, u, :], glu_in[:, u, :], ACT.Sigmoid, scale=1.702).then_inc(act_ready.sem, 1)
            else:
                a.wait_ge(gu_ready.sem, gu_ready.base + NU * e + u + 1)
                if not (isinstance(e, int) and NU * e + u < 2):
                    a.wait_ge(hid_ready.sem, hid_ready.base + NU * e + u - 1)
                a.activation(act_sb[:, u % 2, :], psum[0:H, 2 * (u % 2), :], ACT.Silu).then_inc(act_ready.sem, 1)
            a.wait_ge(hid_ready.sem, hid_ready.base + NU * e + u + 1)
            a.copy(r32(hid2[:, s, 0, ht, nh * 512:nh * 512 + 512]), hid[:, u % 2, :]).then_inc(hid_high.sem, 1)

        def add(e, s):
            a.copy(w_cur_a[:, s, :], w_all[:, bass.ts(e, 1), :].rearrange("p a t -> p (a t)")).then_inc(w_cur_a_ready.sem, 1)
            a.wait_ge(w_cur_a_ready.sem, w_cur_a_ready.base + e + 1)
            a.wait_ge(gp_added.sem, gp_added.base + e + 1)
            for pair in range(2, 4):
                a.wait_ge(dn_ready.sem, dn_ready.base + 4 * e + pair + 5)
                for half in range(2):
                    t = 2 * pair + half
                    last = a.mul(weighted[:, s, t - 4, :], psum[:, 4 + pair, D * half:D * half + D],
                                 w_cur_a[:, s, t:t + 1])
                last.then_inc(dn_weighted.sem, 1)

        for nh in range(2):
            c = slice(nh * 512, nh * 512 + 512)
            a.copy(r32(xnT2[:, 0, :, c]), k.xnT[:, :, c]).then_inc(xn_high.sem, 1)
        prepare_gate_up(0, 0, 0)
        a.wait_ge(shifted_ready.sem, shifted_ready.base + 1)
        a.activation(shifted[:, :, :], shifted[:, :, :], ACT.Exp).then_inc(exp_ready.sem, 1)
        a.preload_act_table(ACT.Sigmoid if kind == "l1" else ACT.Silu)
        a.wait_ge(weights_ready.sem, weights_ready.base + 1)
        run(a, prepare_gate_up, prepare_down, unit, add)

    def gpsimd(g):
        def prepare_gate_up(e, s, turn):
            g.wait_ge(gu_high.sem, gu_high.base + e + 1)
            g.tensor_tensor(r32(w_gu2[:, s, 1]), w_gu[:, s], w_gu2[:, s, 0], ALU.subtract).then_inc(gu_low.sem, 1)

        def prepare_down(e, s, turn):
            g.wait_ge(w_dn_high.sem, w_dn_high.base + e + 1)
            g.tensor_tensor(r32(w_dn2[:, s, 1]), w_dn[:, s], w_dn2[:, s, 0], ALU.subtract).then_inc(w_dn_low.sem, 1)

        def unit(e, s, u):
            ht, nh = divmod(u, 2)
            c = slice(nh * 512, nh * 512 + 512)
            g.wait_ge(hid_high.sem, hid_high.base + NU * e + u + 1)
            g.tensor_tensor(r32(hid2[:, s, 1, ht, c]), hid[:, u % 2, :], hid2[:, s, 0, ht, c], ALU.subtract
                            ).then_inc(hid_low.sem, 1)

        def add(e, s):
            g.wait_ge(dn_weighted.sem, dn_weighted.base + 2 * e + 4)
            g.wait_ge(gp_added.sem, gp_added.base + e + 2)
            g.tensor_tensor(k.x[:, 4:8, :], k.x[:, 4:8, :], weighted[:, s, :, :], ALU.add).then_inc(gp_added.sem, 1)

        for nh in range(2):
            c = slice(nh * 512, nh * 512 + 512)
            g.wait_ge(xn_high.sem, xn_high.base + nh + 1)
            g.tensor_tensor(r32(xnT2[:, 1, :, c]), k.xnT[:, :, c], xnT2[:, 0, :, c], ALU.subtract).then_inc(xn_low.sem, 1)
        prepare_gate_up(0, 0, 0)
        run(g, prepare_gate_up, prepare_down, unit, add)

    return dict(sync=sync, gpsimd=gpsimd, tensor=tensor, vector=vector, scalar=scalar)


def l0_ffn(k):
    return routed_ffn(k, "l0f", 16, 112, 4, 4, "l0")


def l1_ffn(k):
    return routed_ffn(k, "l1f", 32, 128, 1, 4, "l1")


def l2_ffn(k):
    return routed_ffn(k, "l2f", 8, 128, 1, 2, "l2")




def l2_attention(k):
    psum, ins, gate = k.psum, k.ins, k.gate
    NEG, SCALE = -1e30, 1.0 / 16.0
    k.top = 0
    ctx_rows = k.local("l2a_ctx_rows", [S, BATCHES, D])
    mask_in = k.local("l2a_mask_in", [P, TILES * S // 4], I32)
    mask = k.local("l2a_mask", [P, TILES, S])
    off = k.local("l2a_off", [P, TILES, S])
    probs = k.local("l2a_probs", [P, TILES, S])
    stat = k.local("l2a_stat", [P, TILES])
    valid = k.local("l2a_valid", [P, TILES])
    probs_t = k.local("l2a_probs_t", [S, TILES * P])
    loaded, scores_ready, shifted_ready = k.sem("l2a_loaded"), k.sem("l2a_scores_ready"), k.sem("l2a_shifted_ready")
    exp_ready, probs_ready, turned = k.sem("l2a_exp_ready"), k.sem("l2a_probs_ready"), k.sem("l2a_turned")
    turn_copied, read_out = k.sem("l2a_turn_copied"), k.sem("l2a_read_out")

    def sync(sp):
        sp.dma_start(mask_in[:], ins["l2a_mask"]).then_inc(loaded, 16)
        sp.dma_start(ctx_rows[:], ins["ctx"].rearrange("b s d -> s b d")).then_inc(loaded, 16)

    def tensor(pe):
        for b in range(BATCHES):
            t, r, c = b // 2, slice(64 * (b % 2), 64 * (b % 2) + 64), slice(b * S, (b + 1) * S)
            for h in range(2):
                last = pe.matmul(psum[r, 2, t * S:(t + 1) * S], k.xnT[:, h, c], k.ctxT[:, h, c],
                                 start=(h == 0), stop=(h == 1))
        last.then_inc(scores_ready, 1)
        pe.wait_ge(probs_ready, 1)
        for t in range(TILES):
            last = pe.transpose(psum[0:S, 3 + t // 4, (t % 4) * P:(t % 4 + 1) * P], probs[:, t, :], k.ident[:, :])
        last.then_inc(turned, 1)
        pe.wait_ge(turn_copied, 1)
        pe.wait_ge(loaded, 32)
        for b in range(BATCHES):
            t, r = b // 2, slice(64 * (b % 2), 64 * (b % 2) + 64)
            last = pe.matmul(psum[r, 4 + t // 2, D * (t % 2):D * (t % 2) + D], probs_t[:, b * S:(b + 1) * S],
                             ctx_rows[:, b, :], start=True, stop=True)
        last.then_inc(read_out, 1)

    def vector(v, st):
        v.wait_ge(loaded, 32)
        st.link(v.tensor_copy(mask[:, :, :].rearrange("p t s -> p (t s)"), mask_in[:, :].bitcast(U8)))
        v.tensor_reduce(valid[:, :], mask[:, :, :], X, ALU.max)
        st.link(v.tensor_scalar(off[:, :, :], mask[:, :, :], 1.0, -NEG, ALU.subtract, ALU.mult))
        v.wait_ge(scores_ready, 1)
        scores = psum[:, 2, :].rearrange("p (t s) -> p t s", t=TILES)
        st.link(v.tensor_tensor(probs[:, :, :], scores, mask[:, :, :], ALU.mult))
        st.link(v.scalar_tensor_tensor(probs[:, :, :], probs[:, :, :], SCALE, off[:, :, :], ALU.mult, ALU.add))
        st.link(v.tensor_reduce(stat[:, :], probs[:, :, :], X, ALU.max))
        v.tensor_tensor(probs[:, :, :], probs[:, :, :], repeat(stat[:, :], 2, S), ALU.subtract
                        ).then_inc(shifted_ready, 1)
        v.wait_ge(exp_ready, 1)
        st.link(v.tensor_reduce(stat[:, :], probs[:, :, :], X, ALU.add))
        st.link(v.reciprocal(stat[:, :], stat[:, :]))
        st.link(v.tensor_tensor(stat[:, :], stat[:, :], valid[:, :], ALU.mult))
        v.tensor_tensor(probs[:, :, :], probs[:, :, :], repeat(stat[:, :], 2, S), ALU.mult).then_inc(probs_ready, 1)
        v.wait_ge(read_out, 1)
        flat = k.x[:, :, :].rearrange("p t d -> p (t d)")
        st.link(v.scalar_tensor_tensor(flat, k.banks(4, 4), gate, flat, ALU.mult, ALU.add))

    def scalar(a):
        a.wait_ge(shifted_ready, 1)
        a.activation(probs[:, :, :], probs[:, :, :], ACT.Exp).then_inc(exp_ready, 1)
        a.wait_ge(turned, 1)
        a.copy(probs_t[:, :], psum[0:S, 3:5, :].rearrange("p a n -> p (a n)")).then_inc(turn_copied, 1)

    return dict(sync=sync, tensor=tensor, vector=vector, scalar=scalar)




def l1_attention(k):
    psum, ins, gate = k.psum, k.ins, k.gate
    H, HP, QC, L, R = 16, 8, 96, 64, 64
    NEG, SCALE = -1e30, float(1.0 / (192.0 ** 0.5))
    k.top = 0
    w_kvc = k.local("l1a_w_kvc", [P, 2, L])
    w_dq = k.local("l1a_w_dq", [P, 2, QC])
    w_kr = k.local("l1a_w_kr", [L, 2, R])
    w_uq = k.local("l1a_w_uq", [P, H, QC])
    w_uk = k.local("l1a_w_uk", [P, H, L])
    w_uv = k.local("l1a_w_uv", [P, H, L])
    w_o = k.local("l1a_w_o", [P, H, D])
    aq = k.local("l1a_aq", [QC, H, P])
    w_rot = k.local("l1a_w_rot", [QC, H, R])
    b2 = k.local("l1a_b2", [P, HP, D])
    rope = k.local("l1a_rope", [P, 2, S])
    seg_in = k.local("l1a_seg_in", [P, BATCHES], I32)
    seg = k.local("l1a_seg", [P, BATCHES])
    good = k.local("l1a_good", [P, BATCHES, S])
    off = k.local("l1a_off", [P, BATCHES, S])
    kcat = k.local("l1a_kcat", [P, TOKENS])
    rope_a = k.local("l1a_rope_a", [P, 1024])
    rope_b = k.local("l1a_rope_b", [P, 1024])
    kv_diag = k.local("l1a_kv_diag", [P, BATCHES, P])
    qc = k.local("l1a_qc", [QC, TOKENS])
    qc_cur = k.local("l1a_qc_cur", [QC, 2, P])
    kv_cur = k.local("l1a_kv_cur", [P, 2, 2, P])
    q = k.local("l1a_q", [P, 2, 2, H, S])
    probs = k.local("l1a_probs", [P, 2, HP, S])
    stat = k.local("l1a_stat", [P, 2, HP])
    probs_t = k.local("l1a_probs_t", [P, 2, 512])
    o_cat = k.local("l1a_o_cat", [P, HP, 2, S])

    loaded = k.sem("l1a_loaded")
    s_kv, s_kv_c = k.sem("l1a_kv_ready"), k.sem("l1a_kv_copied")
    s_kr, s_kr_c = k.sem("l1a_kr_ready"), k.sem("l1a_kr_roped")
    s_a, s_a_c = k.sem("l1a_fold_a_ready"), k.sem("l1a_fold_a_copied")
    s_b, s_b_c = k.sem("l1a_fold_b_ready"), k.sem("l1a_fold_b_copied")
    s_qc, s_qc_c = k.sem("l1a_qc_ready"), k.sem("l1a_qc_copied")
    zeroed, cur_ready = k.sem("l1a_zeroed"), k.sem("l1a_cur_ready")
    q_ready, q_abs_copied, q_roped = k.sem("l1a_q_ready"), k.sem("l1a_q_abs_copied"), k.sem("l1a_q_roped")
    scores_ready, shifted_ready, exp_ready = (k.sem("l1a_scores_ready"), k.sem("l1a_shifted_ready"),
                                              k.sem("l1a_exp_ready"))
    probs_ready, turned, turn_copied = k.sem("l1a_probs_ready"), k.sem("l1a_turned"), k.sem("l1a_turn_copied")
    av_ready, av_copied, out_ready, added = (k.sem("l1a_av_ready"), k.sem("l1a_av_copied"), k.sem("l1a_out_ready"),
                                             k.sem("l1a_added"))
    loads = [(w_kvc[:], "l1a_w_kvc"), (w_dq[:], "l1a_w_dq"), (w_kr[:], "l1a_w_kr"), (w_uq[:], "l1a_w_uq"),
             (w_uk[:], "l1a_w_uk"), (w_uv[:], "l1a_w_uv"), (w_o[:], "l1a_w_o"), (aq[:, :, L:P], "l1a_w_qr"),
             (w_rot[:], "l1a_w_rot"), (rope[:], "l1a_rope"), (seg_in[:], "l1a_seg")]

    def sync(sp):
        for dst, name in loads:
            sp.dma_start(dst, ins[name]).then_inc(loaded, 16)

    def tensor(pe):
        pe.wait_ge(loaded, 16 * len(loads))
        for n in range(2):
            for h in range(2):
                last = pe.matmul(psum[0:L, n, :], w_kvc[:, h, :], k.ctxT[:, h, n * 512:n * 512 + 512],
                                 start=(h == 0), stop=(h == 1))
        last.then_inc(s_kv, 1)
        for n in range(2):
            for h in range(2):
                last = pe.matmul(psum[0:QC, 2 + n, :], w_dq[:, h, :], k.xnT[:, h, n * 512:n * 512 + 512],
                                 start=(h == 0), stop=(h == 1))
        last.then_inc(s_qc, 1)
        for h in range(H):
            last = pe.matmul(psum[0:QC, 4 + h // 8, (h % 8) * L:(h % 8 + 1) * L], w_uq[:, h, :], w_uk[:, h, :],
                             start=True, stop=True)
        last.then_inc(s_a, 1)
        pe.wait_ge(s_kv_c, 1)
        for b in range(BATCHES):
            for half in (slice(0, S), slice(S, P)):
                last = pe.matmul(psum[half, 6 + b // 8, (b % 8) * L:(b % 8 + 1) * L], kcat[0:L, b * S:(b + 1) * S],
                                 k.ident[0:L, 0:L], start=True, stop=True)
        last.then_inc(s_kv, 1)
        for v in range(2):
            for n in range(2):
                if v == 0:
                    last = pe.matmul(psum[L:P, n, :], w_kr[:, v, :], kcat[0:L, n * 512:n * 512 + 512],
                                     start=True, stop=True)
                else:
                    if n == 0:
                        pe.wait_ge(s_qc_c, 1)
                    last = pe.matmul(psum[L:P, 2 + n, :], w_kr[:, v, :], kcat[0:L, n * 512:n * 512 + 512],
                                     start=True, stop=True)
        last.then_inc(s_kr, 1)
        pe.wait_ge(s_a_c, 1)
        pe.wait_ge(s_kv_c, 2)
        for h in range(H):
            r = slice(64 * (h // 2 % 2), 64 * (h // 2 % 2) + 64)
            last = pe.matmul(psum[r, 4 + h // 4, D * (h % 2):D * (h % 2) + D], w_uv[:, h, :], w_o[:, h, :],
                             start=True, stop=True)
        last.then_inc(s_b, 1)
        pe.wait_ge(s_b_c, 1)
        pe.wait_ge(s_kr_c, 1)

        def queries(t, s, hf):
            pe.wait_ge(cur_ready, t + 1)
            if not (isinstance(t, int) and t == 0 and hf == 0):
                pe.wait_ge(q_abs_copied, 2 * t + hf)
                pe.wait_ge(q_roped, 2 * t + hf)
            for h in range(8):
                pe.matmul(psum[:, h // 4, (h % 4) * P:(h % 4 + 1) * P], aq[:, 8 * hf + h, :], qc_cur[:, s, :],
                          start=True, stop=True)
                last = pe.matmul(psum[L:P, 2 + h // 4, (h % 4) * P:(h % 4 + 1) * P], w_rot[:, 8 * hf + h, :],
                                 qc_cur[:, s, :], start=True, stop=True)
            last.then_inc(q_ready, 1)

        def scores(t, s):
            pe.wait_ge(q_abs_copied, 2 * t + 2)
            pe.wait_ge(q_roped, 2 * t + 2)
            for b in range(2):
                for hp in range(HP):
                    last = pe.matmul(psum[:, 4 + b, hp * S:(hp + 1) * S],
                                     q[:, s, b, 2 * hp:2 * hp + 2, :].rearrange("p h n -> p (h n)"),
                                     k_cur[:, s, b * S:(b + 1) * S], start=True, stop=True)
                last.then_inc(scores_ready, 1)

        def turn(t, s):
            for b in range(2):
                pe.wait_ge(probs_ready, 2 * t + b + 1)
                if b == 0:
                    pe.wait_ge(added, t + 1)
                for j in range(HP // 2):
                    last = pe.transpose(psum[:, 6 + b, j * P:(j + 1) * P],
                                        probs[:, b, 2 * j:2 * j + 2, :].rearrange("p h n -> p (h n)"), k.ident[:, :])
                last.then_inc(turned, 1)

        def attend(t, s):
            for b in range(2):
                pe.wait_ge(turn_copied, 2 * t + b + 1)
                pe.matmul(psum[:, 4 + b, :], kv_cur[:, s, b, :], probs_t[:, b, :], start=True, stop=True
                          ).then_inc(av_ready, 1)

        def project_out(t, s):
            pe.wait_ge(av_copied, 2 * t + 2)
            for hp in range(HP):
                last = pe.matmul(psum[:, 6, 0:D], o_cat[:, hp, :, :].rearrange("p b n -> p (b n)"), b2[:, hp, :],
                                 start=(hp == 0), stop=(hp == HP - 1))
            last.then_inc(out_ready, 1)

        def tile(t, s, more=True):
            scores(t, s)
            if more:
                queries(t + 1, 1 - s, 0)
            turn(t, s)
            attend(t, s)
            if more:
                queries(t + 1, 1 - s, 1)
            project_out(t, s)

        queries(0, 0, 0)
        queries(0, 0, 1)
        with pe.Fori(0, TILES // 2 - 1) as i:
            tile(2 * i, 0)
            tile(2 * i + 1, 1)
        tile(TILES - 2, 0)
        tile(TILES - 1, 1, more=False)

    k_cur = k.local("l1a_k_cur", [P, 2, P])

    def gpsimd(g):
        g.wait_ge(s_qc_c, 1)
        g.wait_ge(s_kr_c, 1)
        g.wait_ge(s_kv_c, 2)
        g.wait_ge(zeroed, 1)

        def stage(t, s):
            if not (isinstance(t, int) and t < 2):
                g.wait_ge(out_ready, t - 1)
            g.tensor_copy(qc_cur[:, s, :], qc[:, bass.ts(t, P)])
            g.tensor_copy(k_cur[:, s, :], kcat[:, bass.ts(t, P)])
            g.tensor_copy(kv_cur[:, s, :, :].rearrange("p b n -> p (b n)"),
                          kv_diag[:, :, :].rearrange("p b n -> p (b n)")[:, bass.ts(t, 2 * P)]).then_inc(cur_ready, 1)

        stage(0, 0)
        stage(1, 1)
        with g.Fori(0, TILES // 2 - 1) as i:
            stage(2 * i + 2, 0)
            stage(2 * i + 3, 1)

    def vector(v, st):
        v.sem_inc(added, 1)
        v.memset(kv_diag[0:S, :, L:P], 0.0)
        v.memset(kv_diag[S:P, :, 0:L], 0.0).then_inc(zeroed, 1)
        v.wait_ge(loaded, 16 * len(loads))
        st.link(v.tensor_copy(seg[:, :], seg_in[:, :]))
        st.link(v.tensor_tensor(off[:, :, :], repeat(k.iota64[:, :], 1, BATCHES), repeat(seg[:, :], 2, S), ALU.subtract))
        st.link(v.tensor_scalar(good[:, :, :], off[:, :, :], 0.0, None, ALU.is_le))
        st.link(v.scalar_tensor_tensor(good[:, :, :], off[:, :, :], -8.0, good[:, :, :], ALU.is_ge, ALU.mult))
        st.link(v.tensor_scalar(off[:, :, :], good[:, :, :], 1.0, -NEG, ALU.subtract, ALU.mult))

        def roped(dst, plain_banks, swapped_banks):
            def view(t):
                return t.rearrange("p (a n) -> p a n", n=S)
            plain = psum[L:P, plain_banks:plain_banks + 2, :].rearrange("p a n -> p (a n)")
            swapped = psum[L:P, swapped_banks:swapped_banks + 2, :].rearrange("p a n -> p (a n)")
            v.tensor_tensor(view(rope_a[L:P, :]), view(plain), repeat(rope[L:P, 0, :], 1, 16), ALU.mult)
            st.link(v.tensor_tensor(view(rope_b[L:P, :]), view(swapped), repeat(rope[L:P, 1, :], 1, 16), ALU.mult))
            return v.tensor_tensor(dst, rope_a[L:P, :] if len(dst.shape) == 2 else
                                   rope_a[L:P, :].rearrange("p (h b n) -> p h b n", b=2, n=S),
                                   rope_b[L:P, :] if len(dst.shape) == 2 else
                                   rope_b[L:P, :].rearrange("p (h b n) -> p h b n", b=2, n=S), ALU.add)

        v.wait_ge(s_kr, 1)
        roped(kcat[L:P, :], 0, 2).then_inc(s_kr_c, 1)

        def queries(t, s, hf):
            v.wait_ge(q_ready, 2 * t + hf + 1)
            roped(q[L:P, s, :, 8 * hf:8 * hf + 8, :].rearrange("p b h n -> p h b n"), 0, 2).then_inc(q_roped, 1)
            v.wait_ge(q_roped, 2 * t + hf + 1)

        def shift(t, s):
            for b in range(2):
                def mine(m):
                    return repeat(m[:, bass.ts(2 * t + b, 1), :].rearrange("p a n -> p (a n)"), 1, HP)
                v.wait_ge(scores_ready, 2 * t + b + 1)
                p = probs[:, b, :, :]
                st.link(v.tensor_tensor(p, psum[:, 4 + b, :].rearrange("p (h n) -> p h n", n=S), mine(good), ALU.mult))
                st.link(v.tensor_tensor(p, p, mine(off), ALU.add))
                st.link(v.tensor_reduce(stat[:, b, :], p, X, ALU.max))
                v.tensor_tensor(p, p, repeat(stat[:, b, :], 2, S), ALU.subtract).then_inc(shifted_ready, 1)

        def divide(t, s):
            for b in range(2):
                p = probs[:, b, :, :]
                v.wait_ge(exp_ready, 2 * t + b + 1)
                st.link(v.tensor_reduce(stat[:, b, :], p, X, ALU.add))
                st.link(v.reciprocal(stat[:, b, :], stat[:, b, :]))
                v.tensor_tensor(p, p, repeat(stat[:, b, :], 2, S), ALU.mult).then_inc(probs_ready, 1)

        def add(t, s):
            v.wait_ge(out_ready, t + 1)
            xt = tile_of(k.x, t)
            v.scalar_tensor_tensor(xt, psum[:, 6, 0:D], gate, xt, ALU.mult, ALU.add).then_inc(added, 1)

        def tile(t, s, more=True):
            shift(t, s)
            divide(t, s)
            if more:
                queries(t + 1, 1 - s, 0)
            if more:
                queries(t + 1, 1 - s, 1)
            add(t, s)

        queries(0, 0, 0)
        queries(0, 0, 1)
        with v.Fori(0, TILES // 2 - 1) as i:
            st.loop(i, 2 * (2 + 10))
            tile(2 * i, 0)
            tile(2 * i + 1, 1)
            st.end(TILES // 2 - 1)
        tile(TILES - 2, 0)
        tile(TILES - 1, 1, more=False)
        v.wait_ge(added, TILES + 1)

    def scalar(a):
        a.wait_ge(s_kv, 1)
        a.copy(kcat[0:L, :], psum[0:L, 0:2, :].rearrange("p a n -> p (a n)")).then_inc(s_kv_c, 1)
        a.wait_ge(s_qc, 1)
        a.copy(qc[:, :], psum[0:QC, 2:4, :].rearrange("p a n -> p (a n)")).then_inc(s_qc_c, 1)
        a.wait_ge(s_a, 1)
        a.copy(aq[:, :, 0:L], psum[0:QC, 4:6, :].rearrange("p a (h n) -> p (a h) n", n=L)).then_inc(s_a_c, 1)
        a.wait_ge(s_kv, 2)
        for half in (slice(0, S), slice(S, P)):
            last = a.copy(kv_diag[half, :, half], psum[half, 6:8, :].rearrange("p a (b n) -> p (a b) n", n=L))
        last.then_inc(s_kv_c, 1)
        a.wait_ge(s_b, 1)
        a.copy(b2[:, :, :].rearrange("p h n -> p (h n)"), k.banks(4, 4)).then_inc(s_b_c, 1)
        a.preload_act_table(ACT.Exp)

        def queries(t, s, hf):
            a.wait_ge(q_ready, 2 * t + hf + 1)
            for b in range(2):
                src = psum[0:L, 0:2, :].rearrange("p a (h b n) -> p (a h) b n", b=2, n=S)
                last = a.copy(q[0:L, s, b, 8 * hf:8 * hf + 8, :], src[:, :, b, :])
            last.then_inc(q_abs_copied, 1)

        def exp(t, s):
            for b in range(2):
                a.wait_ge(shifted_ready, 2 * t + b + 1)
                a.activation(probs[:, b, :, :], probs[:, b, :, :], ACT.Exp, scale=SCALE).then_inc(exp_ready, 1)

        def copies(t, s):
            for b in range(2):
                a.wait_ge(turned, 2 * t + b + 1)
                a.copy(probs_t[:, b, :], psum[:, 6 + b, :]).then_inc(turn_copied, 1)

        def head_outputs(t, s):
            for b in range(2):
                a.wait_ge(av_ready, 2 * t + b + 1)
                a.copy(o_cat[:, :, b, :], psum[:, 4 + b, :].rearrange("p (h n) -> p h n", n=S)).then_inc(av_copied, 1)

        def tile(t, s, more=True):
            exp(t, s)
            if more:
                queries(t + 1, 1 - s, 0)
            copies(t, s)
            head_outputs(t, s)
            if more:
                queries(t + 1, 1 - s, 1)

        queries(0, 0, 0)
        queries(0, 0, 1)
        with a.Fori(0, TILES // 2 - 1) as i:
            tile(2 * i, 0)
            tile(2 * i + 1, 1)
        tile(TILES - 2, 0)
        tile(TILES - 1, 1, more=False)

    return dict(sync=sync, gpsimd=gpsimd, tensor=tensor, vector=vector, scalar=scalar)




def quantise(v, st, y, clipped, power, shifted):
    st.link(v.tensor_scalar(clipped, y, 448.0, -448.0, ALU.min, ALU.max))
    st.link(v.tensor_scalar(power.bitcast(U16), clipped.bitcast(U16), 0x7F80, None, ALU.bitwise_and))
    st.link(v.tensor_scalar(power, power, 2.0 ** -6, 1.5 * 2.0 ** 20, ALU.max, ALU.mult))
    return v.tensor_tensor(shifted, clipped, power, ALU.add)


def l3_attention(k):
    psum, ins, gate = k.psum, k.ins, k.gate
    G, SETS = 8, 4
    SCALE = float(1.0 / P ** 0.5)
    TURN = 2 * TILES
    VALUE_SLOTS = 8
    k.top = 0
    xq = k.local("l3a_xq", [P, SETS, 2, TOKENS])
    vec_in = k.local("l3a_vec_in", [P, 2, 6])
    head_in = k.local("l3a_head_in", [P, 8])
    scal_in = k.local("l3a_scal_in", [P, 6])
    cen = k.local("l3a_cen", [P, P])
    w_scale = k.local("l3a_w_scale", [P, 2, SETS])
    in_recip = k.local("l3a_in_recip", [P, 2, SETS])
    out_scale = k.local("l3a_out_scale", [P, 1])
    y = k.local("l3a_y", [P, 512])
    clipped = k.local("l3a_clipped", [P, 512], BF16)
    power = k.local("l3a_power", [P, 2, 512], BF16)
    shifted = k.local("l3a_shifted", [P, 2, 512])
    raw = k.local("l3a_raw", [P, 2, 6, D])
    raw_v = k.local("l3a_raw_v", [P, 2, 2, 2, P])
    w_out = k.local("l3a_w_out", [P, 2, 4, D])
    smooth = k.local("l3a_smooth", [P, 2, 4])
    smooth_r = k.local("l3a_smooth_r", [P, 2, 4])
    w_q = k.local("l3a_w_q", [P, 2, 2, 2, 512])
    w_k = k.local("l3a_w_k", [P, 2, 2, 2, 512])
    w_out2 = k.local("l3a_w_out2", [P, 2, 2, 4, D])
    ctx2 = k.local("l3a_ctx2", [P, 2, 2, TOKENS])
    proj = k.local("l3a_proj", [P, 2, 6, P])
    squares = k.local("l3a_squares", [P, 2, 6, P])
    ssum = k.local("l3a_ssum", [P, 2, 6])
    rstd = k.local("l3a_rstd", [P, 2, 6])
    normed = k.local("l3a_normed", [P, 2, 6, P])
    values = k.local("l3a_values", [P, VALUE_SLOTS, 2, P])
    q_t = k.local("l3a_q_t", [P, 2, 2, 2, P])
    k_t = k.local("l3a_k_t", [P, 2, 2, P])
    probs = k.local("l3a_probs", [P, 2, 2, P])
    stat = k.local("l3a_stat", [P, 2, 4])
    probs_t = k.local("l3a_probs_t", [P, 2, 2, 2, 2, S])
    cat_q = k.local("l3a_cat_q", [P, 2, 4, P])

    loaded, w_in = k.sem("l3a_loaded"), [k.sem(f"l3a_w_in{s}") for s in range(2)]
    ln_rows, ln_turned, ln_copied = k.sem("l3a_ln_rows"), k.sem("l3a_ln_turned"), k.sem("l3a_ln_copied")
    ln_stats, ln_root = k.sem("l3a_ln_stats"), k.sem("l3a_ln_root")
    xq_shifted, xq_ready, cat_shifted = k.sem("l3a_xq_shifted"), k.sem("l3a_xq_ready"), k.sem("l3a_cat_shifted")
    consts_ready, ctx_ready, zeroed = k.sem("l3a_consts_ready"), k.sem("l3a_ctx_ready"), k.sem("l3a_zeroed")
    w_centred, w_high, w_low = k.sem("l3a_w_centred"), k.sem("l3a_w_high"), k.sem("l3a_w_low")
    wv_ready, out_high, out_low = k.sem("l3a_wv_ready"), k.sem("l3a_out_high"), k.sem("l3a_out_low")
    proj_ready, proj_read = k.sem("l3a_proj_ready"), k.sem("l3a_proj_read")
    squares_ready, ssum_ready = k.sem("l3a_squares_ready"), k.sem("l3a_ssum_ready")
    sum_ready = k.sem("l3a_sum_ready")
    rstd_ready, normed_ready = k.sem("l3a_rstd_ready"), k.sem("l3a_normed_ready")
    turned, turn_copied = k.sem("l3a_turned"), k.sem("l3a_turn_copied")
    scores_ready, shift_ready, exp_ready = k.sem("l3a_scores_ready"), k.sem("l3a_shift_ready"), k.sem("l3a_exp_ready")
    probs_ready, p_turned, p_copied = k.sem("l3a_probs_ready"), k.sem("l3a_p_turned"), k.sem("l3a_p_copied")
    av_ready, av_read, cat_ready = k.sem("l3a_av_ready"), k.sem("l3a_av_read"), k.sem("l3a_cat_ready")
    out_ready, added = k.sem("l3a_out_ready"), k.sem("l3a_added")
    small = [(vec_in[:], ins["l3a_vec"]), (head_in[:], ins["l3a_head"]), (cen[:], ins["cen"])]
    small += [(scal_in[:, n:n + 1], ins[f"l3a_scalar{n}"].partition_broadcast(P)) for n in range(6)]

    def sync(sp):
        for dst, src in small:
            sp.dma_start(dst, src).then_inc(loaded, 16)

        def load(g, s):
            for dst, name in ((raw, "l3a_raw"), (raw_v, "l3a_raw_v"), (w_out, "l3a_w_out"), (smooth, "l3a_smooth")):
                names = " ".join("abc"[:len(dst.shape) - 2])
                sp.dma_start(dst[:, s].rearrange(f"p {names} -> p ({names})"), ins[name][bass.ts(g, 1)].rearrange("e p n -> p (e n)")).then_inc(w_in[s], 16)

        load(0, 0)
        load(1, 1)
        with sp.Fori(0, G // 2 - 1) as i:
            for s in range(2):
                sp.wait_ge(w_low, 6 * (2 * i + s + 1))
                sp.wait_ge(wv_ready, 2 * i + s + 1)
                sp.wait_ge(out_low, 2 * i + s + 1)
                load(2 * i + 2 + s, s)

    XQ_BLOCKS = [(se, h, c) for c in range(0, TOKENS, 512) for se in range(SETS) for h in range(2)]

    XQ_FIRST = len(XQ_BLOCKS) // 2

    def more_inputs(i, n):
        return range(XQ_FIRST + 2 * n, XQ_FIRST + 2 * n + 2) if known(i) and TURN * i + n < XQ_FIRST // 2 else ()

    def four(m, n):
        return m[:, n % 2, :, :].rearrange("p t (b n) -> p (t b) n", b=2)

    UNITS, DEPTH = G * TILES, 8
    CHUNKS = ((w_q, 0, 0), (w_q, P, 0), (w_q, 2 * P, 1), (w_q, 3 * P, 1), (w_k, 0, 2), (w_k, 2 * P, None))

    def known(i):
        return isinstance(i, int)

    def old(i, n, k_):
        return not known(i) or TURN * i + n >= k_

    def steps_of(i, n, table):
        for step, lag in table:
            if not known(i) or 0 <= TURN * i + n - lag < UNITS:
                step(i, n - lag)

    def group_of(i, n):
        g = n // TILES + 1
        return None if known(i) and 2 * i + g >= G else g

    def all_stages(eng, stage, loop=lambda i: None, end=lambda: None):
        for n in range(DEPTH):
            stage(0, n)
        with eng.Fori(0, G // 2 - 1) as i:
            loop(i)
            for n in range(DEPTH, DEPTH + TURN):
                stage(i, n)
            end()
        for n in range(DEPTH, DEPTH + TURN):
            stage(G // 2 - 1, n)

    def tensor(pe):
        for t in range(TILES):
            pe.wait_ge(ln_rows, t + 1)
            if t >= 2:
                pe.wait_ge(ln_copied, t - 1)
            for h in range(2):
                last = pe.transpose(psum[:, t % 2, h * P:(h + 1) * P], k.xn[:, t, h * P:(h + 1) * P], k.ident[:, :])
            last.then_inc(ln_turned, 1)
        pe.wait_ge(loaded, 16 * len(small))
        pe.wait_ge(ln_copied, TILES)
        pe.wait_ge(ctx_ready, 2)

        def centre(i, g, j):
            if j == 0:
                pe.wait_ge(w_in[g % 2], 64 * (i + g // 2 + 1))
            for h in range(2):
                last = pe.matmul(psum[:, 5, 256 + h * P:256 + (h + 1) * P], raw[:, g % 2, j, h * P:(h + 1) * P],
                                 cen[:, :], start=True, stop=True)
            last.then_inc(w_centred, 1)

        for j in range(6):
            if j:
                pe.wait_ge(w_low, j)
            centre(0, 0, j)
        pe.wait_ge(xq_ready, XQ_FIRST)

        def project(i, n):
            s, t = n // TILES % 2, n % TILES
            if t == 0:
                pe.wait_ge(w_low, 6 * (2 * i + n // TILES + 1))
                pe.wait_ge(wv_ready, 2 * i + n // TILES + 1)
            if known(i) and TURN * i + n == TILES // 2:
                pe.wait_ge(xq_ready, len(XQ_BLOCKS))
            if old(i, n, 1):
                pe.wait_ge(proj_read, TURN * i + n)
            c = slice(t * P, (t + 1) * P)
            for bank, cols, lhs, w in ((0, slice(0, 256), 0, w_q), (0, slice(256, 512), 1, w_q),
                                       (1, slice(0, 128), 2, w_k), (1, slice(128, 256), 3, w_k),
                                       (1, slice(256, 512), None, w_k)):
                if lhs is None:
                    pairs = [(ctx2[:, a, h, c], w[:, s, b, h, cols]) for h in range(2) for a, b in PRODUCTS]
                else:
                    pairs = [(xq[:, lhs, h, c], w[:, s, b, h, cols]) for h in range(2) for b in range(2)]
                for m, (lhsT, rhs) in enumerate(pairs):
                    last = pe.matmul(psum[:, bank, cols], r32(lhsT), r32(rhs), start=(m == 0), stop=(m == len(pairs) - 1))
            last.then_inc(proj_ready, 1)

        def turn(i, n):
            pe.wait_ge(normed_ready, TURN * i + n + 1)
            if old(i, n, 1):
                pe.wait_ge(turn_copied, TURN * i + n)
            for j in range(6):
                last = pe.transpose(psum[:, 2 + j // 4, (j % 4) * P:(j % 4 + 1) * P], normed[:, n % 2, j, :],
                                    k.ident[:, :])
            last.then_inc(turned, 1)

        def scores(i, n):
            pe.wait_ge(turn_copied, TURN * i + n + 1)
            if old(i, n, 1):
                pe.wait_ge(shift_ready, TURN * i + n)
            for ty in range(2):
                for b in range(2):
                    last = pe.matmul(psum[:, 4, (2 * ty + b) * S:(2 * ty + b + 1) * S], q_t[:, n % 2, ty, b, :],
                                     k_t[:, n % 2, ty, b * S:(b + 1) * S], start=True, stop=True)
            last.then_inc(scores_ready, 1)

        def turn_probs(i, n):
            pe.wait_ge(probs_ready, TURN * i + n + 1)
            if old(i, n, 1):
                pe.wait_ge(p_copied, TURN * i + n)
            for ty in range(2):
                last = pe.transpose(psum[:, 5, ty * P:(ty + 1) * P], probs[:, n % 2, ty, :], k.ident[:, :])
            last.then_inc(p_turned, 1)

        def attend(i, n):
            pe.wait_ge(p_copied, TURN * i + n + 1)
            if old(i, n, 1):
                pe.wait_ge(av_read, TURN * i + n)
            for ty in range(2):
                last = pe.matmul(psum[:, 6, 256 * ty:256 * ty + 256], values[:, n % VALUE_SLOTS, ty, :],
                                 probs_t[:, n % 2, ty, :, :, :].rearrange("p h b n -> p (h b n)"), start=True, stop=True)
            last.then_inc(av_ready, 1)

        def project_out(i, n):
            if n % TILES == 0:
                pe.wait_ge(out_low, 2 * i + n // TILES + 1)
            pe.wait_ge(cat_ready, TURN * i + n + 1)
            if old(i, n, 1):
                pe.wait_ge(added, TILES + TURN * i + n)
            for j in range(4):
                for part in range(2):
                    last = pe.matmul(psum[:, 7, 0:D], r32(cat_q[:, n % 2, j, :]), r32(w_out2[:, n // TILES % 2, part, j, :]),
                                     start=(j == 0 and part == 0), stop=(j == 3 and part == 1))
            last.then_inc(out_ready, 1)

        def stage(i, n):
            steps_of(i, n, ((project, 0),))
            g, j = group_of(i, n), n % TILES - 1
            if j > 0 and g is not None:
                pe.wait_ge(w_low, 6 * (2 * i + g) + j)
            steps_of(i, n, ((turn_probs, 5), (scores, 3), (turn, 2), (project_out, 7), (attend, 5)))
            if 0 <= j < 6 and g is not None:
                if not (known(i) and TURN * i + n < 5):
                    pe.wait_ge(p_copied, TURN * i + n - 4)
                centre(i, g, j)

        all_stages(pe, stage)

    def gpsimd(g_):
        g_.memset(probs_t[:, :, :, :, :, :], 0.0).then_inc(zeroed, 1)
        g_.wait_ge(ln_stats, 1)
        g_.tensor_tensor(k.rstd[:, :], k.var[:, :], k.minus_half[:, :], ALU.pow).then_inc(ln_root, 1)

        def out_weights(i, g):
            g_.wait_ge(out_high, 2 * i + g + 1)
            g_.tensor_tensor(r32(w_out2[:, g % 2, 1]), w_out[:, g % 2], w_out2[:, g % 2, 0], ALU.subtract
                             ).then_inc(out_low, 1)

        def root(i, n):
            g_.wait_ge(ssum_ready, TURN * i + n + 1)
            g_.tensor_tensor(rstd[:, n % 2, :], ssum[:, n % 2, :], k.minus_half[:, 0:6], ALU.pow).then_inc(rstd_ready, 1)

        def normalise(i, n):
            g_.wait_ge(rstd_ready, TURN * i + n + 1)
            if old(i, n, 2):
                g_.wait_ge(turned, TURN * i + n - 1)
            g_.tensor_tensor(normed[:, n % 2, :, :], proj[:, n % 2, :, :], repeat(rstd[:, n % 2, :], 2, P), ALU.mult
                             ).then_inc(normed_ready, 1)

        def scale_probs(i, n):
            g_.wait_ge(sum_ready, TURN * i + n + 1)
            g_.tensor_tensor(four(probs, n), four(probs, n), repeat(stat[:, n % 2, :], 2, S), ALU.mult
                             ).then_inc(probs_ready, 1)

        def quantised_heads(i, n):
            g_.wait_ge(cat_shifted, TURN * i + n + 1)
            if old(i, n, 2):
                g_.wait_ge(out_ready, TURN * i + n - 1)
            g_.tensor_tensor(r32(cat_q[:, n % 2, :, :].rearrange("p j n -> p (j n)")), shifted[:, n % 2, :],
                             power[:, n % 2, :], ALU.subtract).then_inc(cat_ready, 1)

        def stage(i, n):
            for m in more_inputs(i, n):
                quantised_inputs(m)
            steps_of(i, n, ((quantised_heads, 6), (scale_probs, 4), (root, 1), (normalise, 1)))
            g = group_of(i, n)
            if n % TILES == 7 and g is not None:
                out_weights(i, g)

        out_weights(0, 0)
        def quantised_inputs(m):
            se, h, c = XQ_BLOCKS[m]
            g_.wait_ge(xq_shifted, m + 1)
            g_.tensor_tensor(r32(xq[:, se, h, c:c + 512]), shifted[:, m % 2, :], power[:, m % 2, :], ALU.subtract
                             ).then_inc(xq_ready, 1)

        for m in range(XQ_FIRST):
            quantised_inputs(m)
        all_stages(g_, stage)

    def vector(v, st):
        for t in range(TILES):
            last = v.bn_stats(k.bn[:, t, :], k.xn[:, t, :])
        st.link(last)
        for t in range(TILES):
            last = v.bn_aggr(k.mean_var[:, t, :], k.bn[:, t, :])
        st.link(last)
        v.tensor_scalar(k.var[:, :], k.mean_var[:, :, 1], EPS, None, ALU.add).then_inc(ln_stats, 1)
        v.wait_ge(ln_root, 1)
        for t in range(TILES):
            last = v.tensor_scalar(k.xn[:, t, :], k.xn[:, t, :], k.mean_var[:, t, 0:1], k.rstd[:, t:t + 1],
                                   ALU.subtract, ALU.mult)
            last.then_inc(ln_rows, 1)
        v.wait_ge(loaded, 16 * len(small))
        st.link(v.tensor_tensor(w_scale[:, :, :], vec_in[:, :, 2:6], repeat(scal_in[:, 0:4], 1, 2), ALU.mult))
        st.link(v.reciprocal(in_recip[:, :, :], vec_in[:, :, 2:6]))
        st.link(v.tensor_tensor(out_scale[:, :], scal_in[:, 4:5], scal_in[:, 5:6], ALU.mult))
        st.link(v.tensor_scalar(out_scale[:, :], out_scale[:, :], gate, None, ALU.mult))
        v.sem_inc(consts_ready, 1)
        v.wait_ge(ctx_ready, 1)
        v.tensor_tensor(r32(ctx2[:, 1]), k.ctxT[:, :, :], ctx2[:, 0], ALU.subtract).then_inc(ctx_ready, 1)
        v.wait_ge(ln_copied, TILES)

        def mean_square(i, n):
            v.wait_ge(squares_ready, TURN * i + n + 1)
            st.link(v.tensor_reduce(ssum[:, n % 2, :], squares[:, n % 2, :, :], X, ALU.add))
            v.tensor_scalar(ssum[:, n % 2, :], ssum[:, n % 2, :], 1.0 / P, EPS, ALU.mult, ALU.add
                            ).then_inc(ssum_ready, 1)

        def shift(i, n):
            v.wait_ge(scores_ready, TURN * i + n + 1)
            if old(i, n, 2):
                v.wait_ge(p_turned, TURN * i + n - 1)
                v.wait_ge(probs_ready, TURN * i + n - 1)
            src = psum[:, 4, 0:256].rearrange("p (a n) -> p a n", a=4)
            st.link(v.tensor_reduce(stat[:, n % 2, :], src, X, ALU.max))
            v.tensor_tensor(four(probs, n), src, repeat(stat[:, n % 2, :], 2, S), ALU.subtract).then_inc(shift_ready, 1)

        def divide(i, n):
            v.wait_ge(exp_ready, TURN * i + n + 1)
            st.link(v.tensor_reduce(stat[:, n % 2, :], four(probs, n), X, ALU.add))
            v.reciprocal(stat[:, n % 2, :], stat[:, n % 2, :]).then_inc(sum_ready, 1)

        def quantise_heads(i, n):
            v.wait_ge(av_ready, TURN * i + n + 1)
            v.tensor_tensor(y[:, :].rearrange("p (j n) -> p j n", j=4), psum[:, 6, :].rearrange("p (j n) -> p j n", j=4),
                            repeat(smooth_r[:, n // TILES % 2, :], 2, P), ALU.mult).then_inc(av_read, 1)
            v.wait_ge(av_read, TURN * i + n + 1)
            if old(i, n, 2):
                v.wait_ge(cat_ready, TURN * i + n - 1)
            quantise(v, st, y[:, :], clipped[:, :], power[:, n % 2, :], shifted[:, n % 2, :]).then_inc(cat_shifted, 1)
            v.wait_ge(cat_shifted, TURN * i + n + 1)

        def add(i, n):
            t = n % TILES
            v.wait_ge(out_ready, TURN * i + n + 1)
            v.wait_ge(added, TURN * i + n + 1)
            v.scalar_tensor_tensor(k.x[:, t, :], psum[:, 7, 0:D], out_scale[:, 0:1], k.x[:, t, :], ALU.mult, ALU.add
                                   ).then_inc(added, 1)

        def low_weights(i, g, j):
            s, (dst, col, scale) = g % 2, CHUNKS[j]
            v.wait_ge(w_high, 6 * (2 * i + g) + j + 1)
            if scale is None:
                last = v.tensor_tensor(r32(dst[:, s, 1, :, col:col + P]), psum[:, 5, 256:512].rearrange("p (h n) -> p h n", h=2),
                                       dst[:, s, 0, :, col:col + P], ALU.subtract)
            else:
                for h in range(2):
                    last = v.scalar_tensor_tensor(r32(dst[:, s, 1, h, col:col + P]), psum[:, 5, 256 + h * P:256 + (h + 1) * P],
                                                  w_scale[:, h, scale:scale + 1], dst[:, s, 0, h, col:col + P],
                                                  ALU.mult, ALU.subtract)
            last.then_inc(w_low, 1)

        def value_weights(i, g):
            s = g % 2
            v.wait_ge(w_in[s], 64 * (i + g // 2 + 1))
            if not (known(i) and 2 * i + g < 2):
                v.wait_ge(proj_ready, TILES * (2 * i + g - 1))
            for h in range(2):
                v.tensor_scalar(r32(w_k[:, s, 0, h, P:2 * P]), raw_v[:, s, 0, h, :], w_scale[:, h, 3:4], None, ALU.mult)
            st.link(v.tensor_copy(r32(w_k[:, s, 0, :, 3 * P:4 * P]), raw_v[:, s, 1, :, :]))
            for h in range(2):
                v.scalar_tensor_tensor(r32(w_k[:, s, 1, h, P:2 * P]), raw_v[:, s, 0, h, :], w_scale[:, h, 3:4],
                                       w_k[:, s, 0, h, P:2 * P], ALU.mult, ALU.subtract)
            v.tensor_tensor(r32(w_k[:, s, 1, :, 3 * P:4 * P]), raw_v[:, s, 1, :, :],
                            w_k[:, s, 0, :, 3 * P:4 * P], ALU.subtract).then_inc(wv_ready, 1)

        def smooth_weights(i, g):
            st.link(v.reciprocal(smooth_r[:, g % 2, :], smooth[:, g % 2, :]))

        def stage(i, n):
            for m in more_inputs(i, n):
                quantise_inputs(m)
            steps_of(i, n, ((quantise_heads, 6), (divide, 4), (mean_square, 1), (shift, 3), (add, 7)))
            g, j = group_of(i, n), n % TILES - 1
            if g is None:
                return
            if j == -1:
                value_weights(i, g)
            if j == 5:
                smooth_weights(i, g)
            if 0 <= j < 6:
                low_weights(i, g, j)

        value_weights(0, 0)
        smooth_weights(0, 0)

        def quantise_inputs(m):
            se, h, c = XQ_BLOCKS[m]
            st.link(v.tensor_scalar(y[:, :], k.xnT[:, h, c:c + 512], in_recip[:, h, se:se + 1], None, ALU.mult))
            if m >= 2:
                v.wait_ge(xq_ready, m - 1)
            quantise(v, st, y[:, :], clipped[:, :], power[:, m % 2, :], shifted[:, m % 2, :]).then_inc(xq_shifted, 1)
            v.wait_ge(xq_shifted, m + 1)
            if m == len(XQ_BLOCKS) - 1:
                v.wait_ge(xq_ready, m + 1)

        for m in range(XQ_FIRST):
            quantise_inputs(m)
            if m < 6:
                low_weights(0, 0, m)
        v.sem_inc(added, TILES)
        all_stages(v, stage, lambda i: st.loop(i, TURN * 6 + 2 * 2), lambda: st.end(G // 2 - 1))
        v.wait_ge(added, TILES + UNITS)

    def scalar(a):
        a.copy(r32(ctx2[:, 0]), k.ctxT[:, :, :]).then_inc(ctx_ready, 1)
        a.wait_ge(loaded, 16 * len(small))
        for t in range(TILES):
            a.wait_ge(ln_turned, t + 1)
            for h in range(2):
                last = a.activation(k.xnT[:, h, t * P:(t + 1) * P], psum[:, t % 2, h * P:(h + 1) * P], ACT.Identity,
                                    scale=vec_in[:, h, 0:1], bias=vec_in[:, h, 1:2])
            last.then_inc(ln_copied, 1)
        a.wait_ge(consts_ready, 1)
        a.preload_act_table(ACT.Exp)
        a.wait_ge(zeroed, 1)

        def high_weights(i, g, j):
            s, (dst, col, scale) = g % 2, CHUNKS[j]
            if j == 0 and not (known(i) and 2 * i + g < 2):
                a.wait_ge(proj_ready, TILES * (2 * i + g - 1))
            a.wait_ge(w_centred, 6 * (2 * i + g) + j + 1)
            if scale is None:
                last = a.copy(r32(dst[:, s, 0, :, col:col + P]), psum[:, 5, 256:512].rearrange("p (h n) -> p h n", h=2))
            else:
                for h in range(2):
                    last = a.mul(r32(dst[:, s, 0, h, col:col + P]), psum[:, 5, 256 + h * P:256 + (h + 1) * P],
                                 w_scale[:, h, scale:scale + 1])
            last.then_inc(w_high, 1)

        def out_weights(i, g):
            a.wait_ge(w_in[g % 2], 64 * (i + g // 2 + 1))
            if not (known(i) and 2 * i + g < 2):
                a.wait_ge(out_ready, TILES * (2 * i + g - 1))
            a.copy(r32(w_out2[:, g % 2, 0]), w_out[:, g % 2]).then_inc(out_high, 1)

        def squared(i, n):
            a.wait_ge(proj_ready, TURN * i + n + 1)
            if old(i, n, 2):
                a.wait_ge(normed_ready, TURN * i + n - 1)
            if old(i, n, VALUE_SLOTS):
                a.wait_ge(av_ready, TURN * i + n - VALUE_SLOTS + 1)
            pairs = psum[:, 1, :].rearrange("p (a b d) -> p a b d", a=2, b=2)
            a.copy(proj[:, n % 2, 0:4, :], psum[:, 0, :].rearrange("p (j d) -> p j d", j=4))
            a.copy(values[:, n % VALUE_SLOTS, :, :], pairs[:, :, 1, :])
            a.copy(proj[:, n % 2, 4:6, :], pairs[:, :, 0, :]).then_inc(proj_read, 1)
            a.wait_ge(proj_read, TURN * i + n + 1)
            if old(i, n, 2):
                a.wait_ge(ssum_ready, TURN * i + n - 1)
            a.activation(squares[:, n % 2, :, :], proj[:, n % 2, :, :], ACT.Square).then_inc(squares_ready, 1)

        def queries_keys(i, n):
            a.wait_ge(turned, TURN * i + n + 1)
            if old(i, n, 2):
                a.wait_ge(scores_ready, TURN * i + n - 1)
            for ty in range(2):
                src = psum[:, 2, 256 * ty:256 * ty + 256].rearrange("p (h b n) -> p b h n", h=2, b=2)
                last = a.activation(q_t[:, n % 2, ty, :, :].rearrange("p b (h n) -> p b h n", h=2), src, ACT.Identity,
                                    scale=head_in[:, 2 * ty:2 * ty + 1], bias=head_in[:, 2 * ty + 1:2 * ty + 2])
            for ty in range(2):
                last = a.activation(k_t[:, n % 2, ty, :], psum[:, 3, ty * P:(ty + 1) * P], ACT.Identity,
                                    scale=head_in[:, 4 + 2 * ty:5 + 2 * ty], bias=head_in[:, 5 + 2 * ty:6 + 2 * ty])
            last.then_inc(turn_copied, 1)

        def exp(i, n):
            a.wait_ge(shift_ready, TURN * i + n + 1)
            m = probs[:, n % 2, :, :].rearrange("p t n -> p (t n)")
            a.activation(m, m, ACT.Exp, scale=SCALE).then_inc(exp_ready, 1)

        def probs_copy(i, n):
            a.wait_ge(p_turned, TURN * i + n + 1)
            if old(i, n, 2):
                a.wait_ge(av_ready, TURN * i + n - 1)
            for b in range(2):
                rows = slice(b * S, (b + 1) * S)
                last = a.copy(probs_t[rows, n % 2, :, :, b, :],
                              psum[rows, 5, 0:256].rearrange("p (t h n) -> p t h n", t=2, h=2))
            last.then_inc(p_copied, 1)

        def stage(i, n):
            steps_of(i, n, ((squared, 0), (probs_copy, 5), (queries_keys, 2), (exp, 3)))
            g, j = group_of(i, n), n % TILES - 1
            if g is None:
                return
            if 0 <= j < 6:
                high_weights(i, g, j)
            if j == 6:
                out_weights(i, g)

        out_weights(0, 0)
        for j in range(6):
            high_weights(0, 0, j)
        all_stages(a, stage)

    return dict(sync=sync, gpsimd=gpsimd, tensor=tensor, vector=vector, scalar=scalar)




def l3_ffn(k):
    psum, ins, gate = k.psum, k.ins, k.gate
    CH, W = 256, 2
    UNITS = TOKENS // CH * W
    k.top = 0
    w_gu = k.local("l3f_w_gu", [P, 2, 2, W, 4, P])
    w_dn = k.local("l3f_w_dn", [P, W, 4, D])
    act_sb = k.local("l3f_act", [P, 2, 2, CH])
    h_all = k.local("l3f_h_all", [P, 4, CH])
    mag = k.local("l3f_mag", [P, 4, CH])
    near = k.local("l3f_near", [P, 3, CH], BF16)
    skip = k.local("l3f_skip", [P, 2, CH], BF16)
    far = k.local("l3f_far", [P, CH], BF16)
    rank = k.local("l3f_rank", [P, 4, CH], BF16)
    hid = k.local("l3f_hid", [P, 2, W, 4, CH])
    loaded, gu_ready, act_ready, h_ready = (k.sem("l3f_loaded"), k.sem("l3f_gu_ready"), k.sem("l3f_act_ready"),
                                            k.sem("l3f_h_ready"))
    mag_ready, hid_ready, dn_ready, h_free = (k.sem("l3f_mag_ready"), k.sem("l3f_hid_ready"), k.sem("l3f_dn_ready"),
                                              k.sem("l3f_h_free"))

    def sync(sp):
        sp.dma_start(w_gu[:], ins["l3f_w_gu"]).then_inc(loaded, 16)
        sp.dma_start(w_dn[:], ins["l3f_w_dn"]).then_inc(loaded, 16)

    def tensor(pe):
        pe.wait_ge(loaded, 32)

        def gate_up(n):
            c, w = divmod(n, W)
            for pair in range(2):
                if n:
                    pe.wait_ge(h_ready, 2 * (n - 1) + pair + 1)
                for m in (2 * pair, 2 * pair + 1):
                    for g in range(2):
                        for h in range(2):
                            last = pe.matmul(psum[:, 2 * pair + g, CH * (m % 2):CH * (m % 2) + CH], w_gu[:, h, g, w, m, :],
                                             k.xnT[:, h, c * CH:(c + 1) * CH], start=(h == 0), stop=(h == 1))
                last.then_inc(gu_ready, 1)

        def down(c):
            pe.wait_ge(hid_ready, W * (c + 1))
            for half in range(2):
                for w in range(W):
                    for m in range(4):
                        last = pe.matmul(psum[:, 4 + c, D * half:D * half + D], hid[:, c % 2, w, m, half * P:(half + 1) * P],
                                         w_dn[:, w, m, :], start=(w == 0 and m == 0), stop=(w == W - 1 and m == 3))
            last.then_inc(dn_ready, 1)

        for n in range(UNITS + 2):
            if n < UNITS:
                gate_up(n)
            if n >= 3 and n % 2 == 1:
                down((n - 3) // 2)

    def vector(v, st):
        for n in range(UNITS):
            c, w = divmod(n, W)
            for pair in range(2):
                v.wait_ge(act_ready, 2 * n + pair + 1)
                if n and pair == 0:
                    v.wait_ge(mag_ready, n)
                v.tensor_tensor(h_all[:, 2 * pair:2 * pair + 2, :].rearrange("p m n -> p (m n)"),
                                act_sb[:, pair, :, :].rearrange("p m n -> p (m n)"), psum[:, 2 * pair + 1, :],
                                ALU.mult).then_inc(h_ready, 1)
            v.wait_ge(mag_ready, n + 1)
            v.tensor_tensor(near[:, :, :], mag[:, 1:4, :], mag[:, 0:3, :], ALU.is_gt)
            v.tensor_tensor(skip[:, :, :], mag[:, 2:4, :], mag[:, 0:2, :], ALU.is_gt)
            st.link(v.tensor_tensor(far[:, :], mag[:, 3, :], mag[:, 0, :], ALU.is_gt))
            v.tensor_tensor(rank[:, 0, :], near[:, 0, :], skip[:, 0, :], ALU.add)
            v.tensor_tensor(rank[:, 1, :], near[:, 1, :], skip[:, 1, :], ALU.add)
            v.tensor_tensor(rank[:, 2, :], near[:, 2, :], skip[:, 0, :], ALU.subtract)
            st.link(v.tensor_tensor(rank[:, 3, :], near[:, 2, :], skip[:, 1, :], ALU.add))
            v.tensor_tensor(rank[:, 0, :], rank[:, 0, :], far[:, :], ALU.add)
            v.tensor_tensor(rank[:, 1, :], rank[:, 1, :], near[:, 0, :], ALU.subtract)
            v.tensor_tensor(rank[:, 2, :], rank[:, 2, :], near[:, 1, :], ALU.subtract)
            st.link(v.tensor_tensor(rank[:, 3, :], rank[:, 3, :], far[:, :], ALU.add))
            if c >= 2:
                v.wait_ge(dn_ready, c - 1)
            for m, bound, op in ((0, 2.0, ALU.is_lt), (1, 1.0, ALU.is_lt), (2, 0.0, ALU.is_lt), (3, 1.0, ALU.is_gt)):
                last = v.scalar_tensor_tensor(hid[:, c % 2, w, m, :], rank[:, m, :], bound, h_all[:, m, :], op, ALU.mult)
            last.then_inc(hid_ready, 1)
            v.wait_ge(hid_ready, n + 1)
        v.wait_ge(dn_ready, TOKENS // CH)
        flat = k.x[:, :, :].rearrange("p t d -> p (t d)")
        st.link(v.scalar_tensor_tensor(flat, k.banks(4, 4), gate, flat, ALU.mult, ALU.add))

    def scalar(a):
        for n in range(UNITS):
            for pair in range(2):
                a.wait_ge(gu_ready, 2 * n + pair + 1)
                a.activation(act_sb[:, pair, :, :].rearrange("p m n -> p (m n)"), psum[:, 2 * pair, :], ACT.Silu
                             ).then_inc(act_ready, 1)
            a.wait_ge(h_ready, 2 * n + 2)
            if n:
                a.wait_ge(hid_ready, n)
            a.activation(mag[:, :, :], h_all[:, :, :], ACT.Abs).then_inc(mag_ready, 1)

    return dict(sync=sync, tensor=tensor, vector=vector, scalar=scalar)




def start_stage(k):
    loaded, gates_ready, half_ready = k.sem("start_loaded"), k.sem("start_gates_ready"), k.sem("start_half_ready")
    ins = k.ins

    def sync(sp):
        sp.dma_start(k.x[:], ins["x"].rearrange("(t p) d -> p t d", p=P)).then_inc(loaded, 16)
        sp.dma_start(k.ident[:], ins["ident"]).then_inc(loaded, 16)
        sp.dma_start(k.iota[:], ins["iota"]).then_inc(loaded, 16)
        sp.dma_start(k.iota64[:], ins["iota64"]).then_inc(loaded, 16)
        sp.dma_start(k.ctxT[:], ins["ctx_t"]).then_inc(loaded, 16)
        sp.dma_start(k.gates_in[:, 0:4], ins["g_xattn"].partition_broadcast(P)).then_inc(loaded, 16)
        sp.dma_start(k.gates_in[:, 4:8], ins["g_ffn"].partition_broadcast(P)).then_inc(loaded, 16)

    def tensor(pe):
        pe.wait_ge(loaded, 112)

    def vector(v, st):
        v.wait_ge(loaded, 112)
        v.wait_ge(gates_ready, 1)

    def gpsimd(g):
        g.memset(k.minus_half[:, :], -0.5).then_inc(half_ready, 1)
        g.wait_ge(half_ready, 1)

    def scalar(a):
        a.wait_ge(loaded, 112)
        a.activation(k.gates[:, :], k.gates_in[:, :], ACT.Tanh).then_inc(gates_ready, 1)
        a.wait_ge(gates_ready, 1)

    return dict(sync=sync, gpsimd=gpsimd, tensor=tensor, vector=vector, scalar=scalar)


def end_stage(k):
    stored = k.sem("end_stored")

    def sync(sp):
        sp.wait_ge(k.stage_done, k.stages)
        sp.dma_start(k.out.rearrange("(t p) d -> p t d", p=P), k.x[:]).then_inc(stored, 16)
        sp.wait_ge(stored, 16)

    return dict(sync=sync)


def stage_list(k, which):
    table = [("l0a", lambda k: l0_attention(k), 0, False), ("l0f", lambda k: l0_ffn(k), 4, True),
             ("l1a", lambda k: l1_attention(k), 1, True), ("l1f", lambda k: l1_ffn(k), 5, True),
             ("l2a", lambda k: l2_attention(k), 2, True), ("l2f", lambda k: l2_ffn(k), 6, True),
             ("l3a", lambda k: l3_attention(k), 3, False), ("l3f", lambda k: l3_ffn(k), 7, True)]
    return [table[i] for i in which]


def build(nc, ins, out, which=range(8)):
    with ExitStack() as ctx:
        k = Kit(nc, ctx, ins, out)
        k.x = k.sb("x", [P, TILES, D])
        k.xn = k.sb("xn", [P, TILES, D])
        k.xnT = k.sb("xnT", [P, 2, TOKENS])
        k.ident = k.sb("ident", [P, P])
        k.iota = k.sb("iota", [P, 32])
        k.iota64 = k.sb("iota64", [P, S])
        k.ctxT = k.sb("ctxT", [P, 2, TOKENS])
        k.gates_in, k.gates = k.sb("gates_in", [P, 8]), k.sb("gates", [P, 8])
        k.minus_half, k.var, k.rstd = (k.sb(name, [P, TILES]) for name in ("minus_half", "var", "rstd"))
        k.bn, k.mean_var = k.sb("bn", [P, TILES, 6]), k.sb("mean_var", [P, TILES, 2])
        k.base = (nc.sbuf_base + 31) // 32 * 32
        k.stage_done = k.sem("stage_done")
        dve_step = k.sem("dve_step")
        first = start_stage(k)
        stages = []
        for n, (name, make, gate, feature_major) in enumerate(stage_list(k, which)):
            k.gate = k.gates[:, gate:gate + 1]
            norm = norm_stage(k, name, feature_major)
            stages.append((norm, make(k)))
        k.stages = len(stages)
        last = end_stage(k)

        block = ctx.enter_context(nc.Block())

        @block.sync
        def _(sp):
            first["sync"](sp)
            for n, (norm, stage) in enumerate(stages):
                if n:
                    sp.wait_ge(k.stage_done, n)
                if "sync" in stage:
                    stage["sync"](sp)
            last["sync"](sp)

        @block.gpsimd
        def _(g):
            first["gpsimd"](g)
            for n, (norm, stage) in enumerate(stages):
                if n:
                    g.wait_ge(k.stage_done, n)
                norm["gpsimd"](g)
                if "gpsimd" in stage:
                    stage["gpsimd"](g)

        @block.tensor
        def _(pe):
            first["tensor"](pe)
            for n, (norm, stage) in enumerate(stages):
                if n:
                    pe.wait_ge(k.stage_done, n)
                norm["tensor"](pe)
                stage["tensor"](pe)

        @block.vector
        def _(v):
            st = Steps(v, dve_step)
            first["vector"](v, st)
            for n, (norm, stage) in enumerate(stages):
                norm["vector"](v, st)
                stage["vector"](v, st)
                v.sem_inc(k.stage_done, 1)

        @block.scalar
        def _(a):
            first["scalar"](a)
            for n, (norm, stage) in enumerate(stages):
                if n:
                    a.wait_ge(k.stage_done, n)
                norm["scalar"](a)
                stage["scalar"](a)


def host_arrays(inputs):
    import numpy as np

    a = {n: np.asarray(v) for n, v in inputs.items()}
    c = {}
    c["x"] = a["x"].reshape(TOKENS, D)
    c["ctx"] = a["ctx_2048"]
    c["ident"] = np.eye(P, dtype=np.float32)
    c["g_xattn"], c["g_ffn"] = a["g_xattn"], a["g_ffn"]

    def heads(w, n):
        return w.reshape(n, -1, w.shape[1]).transpose(1, 0, 2)

    wq = heads(a["L0_xattn_Wq"], 8)
    c["l0_wq"] = np.concatenate([wq, wq], 2)
    c["l0_wk"] = heads(a["L0_xattn_Wkv"][:512], 8)
    c["l0_wv"] = heads(a["L0_xattn_Wkv"][512:], 8)
    c["l0_wo"] = heads(a["L0_xattn_Wout"].T, 8)
    def gate_up(g, u):
        w = np.stack([g, u], 1).reshape(g.shape[0], 2, g.shape[1], 2, P)
        return w.transpose(0, 4, 3, 1, 2).reshape(g.shape[0], P, -1)

    def down(w, rows):
        return w.reshape(w.shape[0], -1, rows, D).transpose(0, 2, 1, 3).reshape(w.shape[0], rows, -1)

    def feature_halves(w):
        return w.reshape(2, P, -1).transpose(1, 0, 2)

    c["l0f_w_gu"] = gate_up(a["L0_ffn_W_gate"], a["L0_ffn_W_up"])
    c["l0f_w_dn"] = down(a["L0_ffn_W_down"].transpose(0, 2, 1), 112)
    c["l0f_gate_w"] = feature_halves(a["L0_ffn_gate_inp"].T)
    c["l1f_w_gu"] = gate_up(a["L1_ffn_w_gate"].transpose(0, 2, 1), a["L1_ffn_w_up"].transpose(0, 2, 1))
    c["l1f_w_dn"] = down(a["L1_ffn_w_down"], P)
    c["l1f_gate_w"] = feature_halves(a["L1_ffn_gate_w"].T)
    c["l1_gate_b"] = a["L1_ffn_gate_b"]
    c["l1_bias"] = np.stack([a["L1_ffn_b_gate"].T, a["L1_ffn_b_up"].T], 2)
    c["l1_b_down"] = a["L1_ffn_b_down"]
    c["l2f_w_gu"] = gate_up(a["L2_ffn_gate_w"], a["L2_ffn_up_w"])
    c["l2f_w_dn"] = down(a["L2_ffn_down_w"].transpose(0, 2, 1), P)
    c["l2f_gate_w"] = feature_halves(a["L2_ffn_classifier_w"].T)
    c["l2_score_b"] = a["L2_ffn_e_score_correction_bias"]
    c["ctx_t"] = feature_halves(a["ctx_2048"].reshape(TOKENS, D).T)
    mask = a["mask_BxS2_bk0"].view(np.uint8)
    rows = np.repeat(mask.reshape(TILES, 2, S), S, axis=1).transpose(1, 0, 2)
    c["l2a_mask"] = np.ascontiguousarray(rows).view(np.int32).reshape(P, -1)

    half = 32
    swap = np.r_[half:2 * half, 0:half]
    c["l1a_w_kvc"] = feature_halves(a["L1_xattn_W_kvc"])
    c["l1a_w_dq"] = feature_halves(a["L1_xattn_W_dq"])
    c["l1a_w_kr"] = np.stack([a["L1_xattn_W_kr"], a["L1_xattn_W_kr"][:, swap]], 1)
    for n in ("uq", "uk", "uv"):
        c["l1a_w_" + n] = a["L1_xattn_W_" + n].reshape(-1, 16, P).transpose(2, 1, 0)
    c["l1a_w_o"] = a["L1_xattn_W_o"].reshape(16, P, D).transpose(1, 0, 2)
    c["l1a_w_qr"] = a["L1_xattn_W_qr"].reshape(96, 16, 64)
    c["l1a_w_rot"] = c["l1a_w_qr"][:, :, swap]
    freq = 1.0 / 10000.0 ** (np.arange(half, dtype=np.float32) / np.float32(half))
    angle = (np.arange(S, dtype=np.float32)[:, None] * freq.astype(np.float32)).astype(np.float32)
    cos, sin = np.cos(angle).T, np.sin(angle).T
    rope = np.stack([np.concatenate([cos, cos]), np.concatenate([-sin, sin])], 1).astype(np.float32)
    c["l1a_rope"] = np.concatenate([rope, rope])
    c["l1a_seg"] = np.concatenate([a["itok_BxS_0_1023"].T] * 2)
    c["cen"] = (np.eye(P) - 1.0 / P).astype(np.float32)
    scales = [a["L3_xattn_" + n + "_in_scale"] for n in ("q", "qx", "k", "v")]
    c["l3a_vec"] = np.stack([a["L3_xattn_ln_w"], a["L3_xattn_ln_b"]] + scales, 1).reshape(2, P, 6).transpose(1, 0, 2)
    c["l3a_head"] = np.stack([a[f"L3_xattn_{n}ln_{z}"] for n in ("q", "qx", "k", "kx") for z in "wb"], 1)
    for n, name in enumerate(("wq_scale", "wqx_scale", "wk_scale", "wv_scale", "proj_w_scale", "proj_in_scale")):
        c[f"l3a_scalar{n}"] = a["L3_xattn_" + name].reshape(1)
    kx, vx = a["L3_xattn_w_kv_x"].reshape(2, 8, P, D)
    rows = [a["L3_xattn_wq"].reshape(8, 2, P, D), a["L3_xattn_wqx"].reshape(8, 2, P, D),
            a["L3_xattn_wk"].reshape(8, 1, P, D), kx[:, None]]
    c["l3a_raw"] = np.concatenate(rows, 1).transpose(0, 2, 1, 3).reshape(8, P, -1)
    both = np.stack([a["L3_xattn_wv"].reshape(8, P, D), vx], 1)
    c["l3a_raw_v"] = both.reshape(8, 2, P, 2, P).transpose(0, 4, 1, 3, 2).reshape(8, P, -1)
    w_out = a["L3_xattn_wproj"].T.reshape(2, 8, 2, P, D).transpose(1, 3, 0, 2, 4)
    c["l3a_w_out"] = w_out.reshape(8, P, -1)
    c["l3a_smooth"] = a["L3_xattn_proj_smooth"].reshape(2, 8, 2, P).transpose(1, 3, 0, 2).reshape(8, P, 4)
    gu = np.stack([a["L3_ffn_w_gate"], a["L3_ffn_w_up"]], 0).reshape(2, 2, P, 2, P, 4)
    c["l3f_w_gu"] = gu.transpose(2, 1, 0, 3, 5, 4)
    c["l3f_w_dn"] = a["L3_ffn_w_down"].reshape(2, P, 4, D).transpose(1, 0, 2, 3)
    c["iota64"] = np.tile(np.arange(64, dtype=np.float32), (P, 1))
    c["iota"] = np.tile(np.arange(32, dtype=np.float32), (P, 1))
    c["l0_bout"] = np.concatenate([a["L0_xattn_bout"]] * 2)[:, None]
    return {n: np.ascontiguousarray(v) for n, v in c.items()}


def kernel(**inputs):
    import numpy as np
    import concourse.bacc as bacc
    from concourse.bass_utils import run_bass_kernel_spmd

    nc = bacc.Bacc("TRN2", target_bir_lowering=False, num_devices=1)
    arrays = host_arrays(inputs)
    aps = {n: nc.dram_tensor("in_" + n, v.shape, mybir.dt.from_np(v.dtype), kind="ExternalInput").ap()
           for n, v in arrays.items()}
    out = nc.dram_tensor("out", (TOKENS, D), F32, kind="ExternalOutput").ap()
    build(nc, aps, out)
    r = run_bass_kernel_spmd(nc, [{"in_" + n: v for n, v in arrays.items()}], core_ids=[0])
    return r.results[0]["out"].reshape(inputs["x"].shape)
```
